# Optimizing a Trainium2 kernel written in Bass

```python
import numpy as np
import jax
import jax.numpy as jnp

def _softmax(x, axis=-1):
    return jax.nn.softmax(x, axis=axis)

def _gelu(x):
    return jax.nn.gelu(x, approximate=True)

def _silu(x):
    return jax.nn.silu(x)

def _sigmoid(x):
    return jax.nn.sigmoid(x)

def _layernorm(x, axis=-1, eps=1e-05):
    m = jnp.mean(x, axis=axis, keepdims=True)
    v = jnp.var(x, axis=axis, keepdims=True)
    return (x - m) / jnp.sqrt(v + eps)

def _scatter_add(tgt, idx, src, axis=0):
    return tgt.at[idx].add(src)

def _segment_sum(src, seg, n):
    return jax.ops.segment_sum(src, seg, n)
kernel_name = 'mk_prb_d1_jaxref_r8_dc0188'

def setup_inputs(seed: int=0):
    np.random.seed(seed)
    _w = jnp.asarray

    def _L0_attn_setup():
        import jax, jax.numpy as jnp
        import numpy as np
        B, S, D = (4, 512, 128)
        H = 8
        DK = D // H
        DV = D // H
        KLEPE = 5
        ROPE_BASE = 10000.0

        def rotate_half(x):
            x1, x2 = jnp.split(x, 2, axis=-1)
            return jnp.concatenate([-x2, x1], axis=-1)

        def rope_sin_cos(seq_len, dim):
            inv_freq = 1.0 / ROPE_BASE ** (jnp.arange(0, dim, 2, dtype=jnp.float32) / dim)
            freqs = jnp.arange(seq_len, dtype=jnp.float32)[:, None] * inv_freq[None, :]
            emb = jnp.concatenate([freqs, freqs], axis=-1)
            return (jnp.sin(emb), jnp.cos(emb))

        def mala_attn(q, k, v):
            sin, cos = rope_sin_cos(q.shape[1], q.shape[-1])
            sin, cos = (sin[None, :, None, :], cos[None, :, None, :])
            q = q * cos + rotate_half(q) * sin
            k = k * cos + rotate_half(k) * sin
            scale = q.shape[-1] ** (-0.5)
            seq_len = q.shape[1]
            kv = jnp.einsum('bshd,bshe->bhde', k, v)
            ksum = k.sum(axis=1)
            vsum = v.sum(axis=1)
            num = jnp.einsum('bshd,bhde->bshe', q, kv) * scale + vsum[:, None, :, :]
            den = jnp.einsum('bshd,bhd->bsh', q, ksum) * scale + seq_len
            return num / den[..., None]

        def lepe_conv(v, w, b):
            Bb, Ss = (v.shape[0], v.shape[1])
            x = v.transpose(0, 2, 3, 1).reshape(Bb, H * DV, Ss)
            y = jax.lax.conv_general_dilated(x, w, window_strides=(1,), padding=[(KLEPE // 2, KLEPE // 2)], dimension_numbers=('NCH', 'OIH', 'NCH'), feature_group_count=H * DV)
            y = y + b[None, :, None]
            return y.reshape(Bb, H, DV, Ss).transpose(0, 3, 1, 2)
        key = jax.random.key(seed)
        ks = jax.random.split(key, 8)
        w = 0.02
        return {'hidden_states': jax.random.normal(ks[0], (B, S, D), dtype=jnp.float32), 'Wq': jax.random.normal(ks[1], (D, D), dtype=jnp.float32) * w, 'Wk': jax.random.normal(ks[2], (D, D), dtype=jnp.float32) * w, 'Wv': jax.random.normal(ks[3], (D, D), dtype=jnp.float32) * w, 'Wg': jax.random.normal(ks[4], (D, D), dtype=jnp.float32) * w, 'Wo': jax.random.normal(ks[5], (D, D), dtype=jnp.float32) * w, 'lepe_w': jax.random.normal(ks[6], (D, 1, KLEPE), dtype=jnp.float32) * 0.1, 'lepe_b': jnp.zeros((D,), dtype=jnp.float32)}
    _L0_attn_in = _L0_attn_setup()

    def _L0_ffn_setup():
        import jax, jax.numpy as jnp
        import numpy as np
        DIM = 128
        DEPTH = 6
        HEADS = 16
        DIM_HEAD = 64
        WINDOW = 32
        INNER = HEADS * DIM_HEAD
        DIM_INNER = int(DIM * 4 * 2 / 3)
        QK_SCALE = 8.0

        def shift_tokens(t):
            a, s = jnp.split(t, 2, -1)
            s = jnp.pad(s, ((0, 0), (1, 0), (0, 0)))[:, :-1]
            return jnp.concatenate([a, s], -1)

        def l2norm(t):
            return t / jnp.maximum(jnp.linalg.norm(t, axis=-1, keepdims=True), 1e-12)

        def rotate_half(x):
            x1, x2 = jnp.split(x, 2, -1)
            return jnp.concatenate([-x2, x1], -1)

        def rotary_tables(n):
            half = jnp.arange(0, DIM_HEAD, 2, dtype=jnp.float32)
            inv_freq = 1.0 / 10000.0 ** (half / DIM_HEAD)
            t = jnp.arange(n, dtype=jnp.float32)
            freqs = t[:, None] * inv_freq[None, :]
            freqs = jnp.concatenate([freqs, freqs], -1)
            base_scale = (half + 0.4 * DIM_HEAD) / (1.4 * DIM_HEAD)
            power = (t - n // 2) / (WINDOW // 2)
            scale = base_scale[None, :] ** power[:, None]
            scale = jnp.concatenate([scale, scale], -1)
            return (freqs, scale)

        def local_attention(q, k, v):
            b, h, n, d = q.shape
            w = WINDOW
            nw = n // w
            bq = q.reshape(b, h, nw, w, d)
            bk = k.reshape(b, h, nw, w, d)
            bv = v.reshape(b, h, nw, w, d)

            def look(t):
                p = jnp.pad(t, ((0, 0), (0, 0), (1, 0), (0, 0), (0, 0)))
                return jnp.concatenate([p[:, :, :nw], p[:, :, 1:]], axis=3)
            bk2, bv2 = (look(bk), look(bv))
            seq = jnp.arange(n).reshape(nw, w)
            seq_p = jnp.pad(seq, ((1, 0), (0, 0)), constant_values=-1)
            jt = jnp.concatenate([seq_p[:nw], seq_p[1:]], axis=1)
            it = seq[:, :, None]
            jb = jt[:, None, :]
            mask = (it < jb) | (it > jb + w) | (jb == -1)
            sim = jnp.einsum('bhwie,bhwje->bhwij', bq, bk2) * QK_SCALE
            sim = jnp.where(mask, -jnp.finfo(sim.dtype).max, sim)
            attn = jax.nn.softmax(sim, -1)
            out = jnp.einsum('bhwij,bhwje->bhwie', attn, bv2)
            return out.reshape(b, h, n, d)

        def attn_layer(x, Wqkv, qs, ksc, Wo):
            b, n, _ = x.shape
            qkv = x @ Wqkv
            q, k, v = jnp.split(qkv, 3, -1)
            sh = lambda t: t.reshape(b, n, HEADS, DIM_HEAD).transpose(0, 2, 1, 3)
            q, k, v = (sh(q), sh(k), sh(v))
            q = l2norm(q) * qs
            k = l2norm(k) * ksc
            freqs, scale = rotary_tables(n)
            cos, sin = (jnp.cos(freqs), jnp.sin(freqs))
            q = q * cos * scale + rotate_half(q) * sin * scale
            inv = 1.0 / scale
            k = k * cos * inv + rotate_half(k) * sin * inv
            out = local_attention(q, k, v)
            out = out.transpose(0, 2, 1, 3).reshape(b, n, INNER)
            return out @ Wo

        def ffn_layer(x, g, bln, W1, b1, W2, b2):
            mu = x.mean(-1, keepdims=True)
            var = ((x - mu) ** 2).mean(-1, keepdims=True)
            xn = (x - mu) / jnp.sqrt(var + 1e-05) * g + bln
            hg = xn @ W1 + b1
            a, gate = jnp.split(hg, 2, -1)
            return a * jax.nn.gelu(gate, approximate=False) @ W2 + b2
        key = jax.random.key(seed)
        ks = jax.random.split(key, 8)
        B, N = (2, 256)
        init = lambda k, shape: jax.random.normal(k, shape, jnp.float32) * 0.02
        return {'x': jax.random.normal(ks[0], (B, N, DIM), jnp.float32), 'Wqkv': init(ks[1], (DEPTH, DIM, 3 * INNER)), 'q_scale': jnp.ones((DEPTH, DIM_HEAD), jnp.float32), 'k_scale': jnp.ones((DEPTH, DIM_HEAD), jnp.float32), 'Wo': init(ks[2], (DEPTH, INNER, DIM)), 'ln_g': jnp.ones((DEPTH, DIM), jnp.float32), 'ln_b': jnp.zeros((DEPTH, DIM), jnp.float32), 'W1': init(ks[3], (DEPTH, DIM, 2 * DIM_INNER)), 'b1': jnp.zeros((DEPTH, 2 * DIM_INNER), jnp.float32), 'W2': init(ks[4], (DEPTH, DIM_INNER, DIM)), 'b2': jnp.zeros((DEPTH, DIM), jnp.float32)}
    _L0_ffn_in = _L0_ffn_setup()
    _d = {'L0_attn_hidden_states': _L0_attn_in['hidden_states'], 'L0_attn_Wq': _L0_attn_in['Wq'], 'L0_attn_Wk': _L0_attn_in['Wk'], 'L0_attn_Wv': _L0_attn_in['Wv'], 'L0_attn_Wg': _L0_attn_in['Wg'], 'L0_attn_Wo': _L0_attn_in['Wo'], 'L0_attn_lepe_w': _L0_attn_in['lepe_w'], 'L0_attn_lepe_b': _L0_attn_in['lepe_b'], 'L0_ffn_Wqkv': _L0_ffn_in['Wqkv'], 'L0_ffn_q_scale': _L0_ffn_in['q_scale'], 'L0_ffn_k_scale': _L0_ffn_in['k_scale'], 'L0_ffn_Wo': _L0_ffn_in['Wo'], 'L0_ffn_ln_g': _L0_ffn_in['ln_g'], 'L0_ffn_ln_b': _L0_ffn_in['ln_b'], 'L0_ffn_W1': _L0_ffn_in['W1'], 'L0_ffn_b1': _L0_ffn_in['b1'], 'L0_ffn_W2': _L0_ffn_in['W2'], 'L0_ffn_b2': _L0_ffn_in['b2']}
    _x0 = _d['L0_attn_hidden_states']
    _d['L0_attn_hidden_states'] = jax.random.normal(jax.random.fold_in(jax.random.key(seed), 1), (1, 2048, 128), dtype=_x0.dtype)
    del _x0
    return _d

def reference(L0_attn_hidden_states, L0_attn_Wq, L0_attn_Wk, L0_attn_Wv, L0_attn_Wg, L0_attn_Wo, L0_attn_lepe_w, L0_attn_lepe_b, L0_ffn_Wqkv, L0_ffn_q_scale, L0_ffn_k_scale, L0_ffn_Wo, L0_ffn_ln_g, L0_ffn_ln_b, L0_ffn_W1, L0_ffn_b1, L0_ffn_W2, L0_ffn_b2):

    def _L0_attn_ref(hidden_states, Wq, Wk, Wv, Wg, Wo, lepe_w, lepe_b):
        import jax, jax.numpy as jnp
        import numpy as np
        B, S, D = (4, 512, 128)
        H = 8
        DK = D // H
        DV = D // H
        KLEPE = 5
        ROPE_BASE = 10000.0

        def rotate_half(x):
            x1, x2 = jnp.split(x, 2, axis=-1)
            return jnp.concatenate([-x2, x1], axis=-1)

        def rope_sin_cos(seq_len, dim):
            inv_freq = 1.0 / ROPE_BASE ** (jnp.arange(0, dim, 2, dtype=jnp.float32) / dim)
            freqs = jnp.arange(seq_len, dtype=jnp.float32)[:, None] * inv_freq[None, :]
            emb = jnp.concatenate([freqs, freqs], axis=-1)
            return (jnp.sin(emb), jnp.cos(emb))

        def mala_attn(q, k, v):
            sin, cos = rope_sin_cos(q.shape[1], q.shape[-1])
            sin, cos = (sin[None, :, None, :], cos[None, :, None, :])
            q = q * cos + rotate_half(q) * sin
            k = k * cos + rotate_half(k) * sin
            scale = q.shape[-1] ** (-0.5)
            seq_len = q.shape[1]
            kv = jnp.einsum('bshd,bshe->bhde', k, v)
            ksum = k.sum(axis=1)
            vsum = v.sum(axis=1)
            num = jnp.einsum('bshd,bhde->bshe', q, kv) * scale + vsum[:, None, :, :]
            den = jnp.einsum('bshd,bhd->bsh', q, ksum) * scale + seq_len
            return num / den[..., None]

        def lepe_conv(v, w, b):
            Bb, Ss = (v.shape[0], v.shape[1])
            x = v.transpose(0, 2, 3, 1).reshape(Bb, H * DV, Ss)
            y = jax.lax.conv_general_dilated(x, w, window_strides=(1,), padding=[(KLEPE // 2, KLEPE // 2)], dimension_numbers=('NCH', 'OIH', 'NCH'), feature_group_count=H * DV)
            y = y + b[None, :, None]
            return y.reshape(Bb, H, DV, Ss).transpose(0, 3, 1, 2)
        Bb, Ss, _ = hidden_states.shape
        q = (hidden_states @ Wq.T).reshape(Bb, Ss, H, DK)
        k = (hidden_states @ Wk.T).reshape(Bb, Ss, H, DK)
        v = (hidden_states @ Wv.T).reshape(Bb, Ss, H, DV)
        o_gate = hidden_states @ Wg.T
        o = mala_attn(q, k, v) + lepe_conv(v, lepe_w, lepe_b)
        o = o.reshape(Bb, Ss, H * DV) * o_gate
        return o @ Wo.T

    def _L0_ffn_ref(x, Wqkv, q_scale, k_scale, Wo, ln_g, ln_b, W1, b1, W2, b2):
        import jax, jax.numpy as jnp
        import numpy as np
        DIM = 128
        DEPTH = 6
        HEADS = 16
        DIM_HEAD = 64
        WINDOW = 32
        INNER = HEADS * DIM_HEAD
        DIM_INNER = int(DIM * 4 * 2 / 3)
        QK_SCALE = 8.0

        def shift_tokens(t):
            a, s = jnp.split(t, 2, -1)
            s = jnp.pad(s, ((0, 0), (1, 0), (0, 0)))[:, :-1]
            return jnp.concatenate([a, s], -1)

        def l2norm(t):
            return t / jnp.maximum(jnp.linalg.norm(t, axis=-1, keepdims=True), 1e-12)

        def rotate_half(x):
            x1, x2 = jnp.split(x, 2, -1)
            return jnp.concatenate([-x2, x1], -1)

        def rotary_tables(n):
            half = jnp.arange(0, DIM_HEAD, 2, dtype=jnp.float32)
            inv_freq = 1.0 / 10000.0 ** (half / DIM_HEAD)
            t = jnp.arange(n, dtype=jnp.float32)
            freqs = t[:, None] * inv_freq[None, :]
            freqs = jnp.concatenate([freqs, freqs], -1)
            base_scale = (half + 0.4 * DIM_HEAD) / (1.4 * DIM_HEAD)
            power = (t - n // 2) / (WINDOW // 2)
            scale = base_scale[None, :] ** power[:, None]
            scale = jnp.concatenate([scale, scale], -1)
            return (freqs, scale)

        def local_attention(q, k, v):
            b, h, n, d = q.shape
            w = WINDOW
            nw = n // w
            bq = q.reshape(b, h, nw, w, d)
            bk = k.reshape(b, h, nw, w, d)
            bv = v.reshape(b, h, nw, w, d)

            def look(t):
                p = jnp.pad(t, ((0, 0), (0, 0), (1, 0), (0, 0), (0, 0)))
                return jnp.concatenate([p[:, :, :nw], p[:, :, 1:]], axis=3)
            bk2, bv2 = (look(bk), look(bv))
            seq = jnp.arange(n).reshape(nw, w)
            seq_p = jnp.pad(seq, ((1, 0), (0, 0)), constant_values=-1)
            jt = jnp.concatenate([seq_p[:nw], seq_p[1:]], axis=1)
            it = seq[:, :, None]
            jb = jt[:, None, :]
            mask = (it < jb) | (it > jb + w) | (jb == -1)
            sim = jnp.einsum('bhwie,bhwje->bhwij', bq, bk2) * QK_SCALE
            sim = jnp.where(mask, -jnp.finfo(sim.dtype).max, sim)
            attn = jax.nn.softmax(sim, -1)
            out = jnp.einsum('bhwij,bhwje->bhwie', attn, bv2)
            return out.reshape(b, h, n, d)

        def attn_layer(x, Wqkv, qs, ksc, Wo):
            b, n, _ = x.shape
            qkv = x @ Wqkv
            q, k, v = jnp.split(qkv, 3, -1)
            sh = lambda t: t.reshape(b, n, HEADS, DIM_HEAD).transpose(0, 2, 1, 3)
            q, k, v = (sh(q), sh(k), sh(v))
            q = l2norm(q) * qs
            k = l2norm(k) * ksc
            freqs, scale = rotary_tables(n)
            cos, sin = (jnp.cos(freqs), jnp.sin(freqs))
            q = q * cos * scale + rotate_half(q) * sin * scale
            inv = 1.0 / scale
            k = k * cos * inv + rotate_half(k) * sin * inv
            out = local_attention(q, k, v)
            out = out.transpose(0, 2, 1, 3).reshape(b, n, INNER)
            return out @ Wo

        def ffn_layer(x, g, bln, W1, b1, W2, b2):
            mu = x.mean(-1, keepdims=True)
            var = ((x - mu) ** 2).mean(-1, keepdims=True)
            xn = (x - mu) / jnp.sqrt(var + 1e-05) * g + bln
            hg = xn @ W1 + b1
            a, gate = jnp.split(hg, 2, -1)
            return a * jax.nn.gelu(gate, approximate=False) @ W2 + b2
        for i in range(DEPTH):
            x = attn_layer(shift_tokens(x), Wqkv[i], q_scale[i], k_scale[i], Wo[i]) + x
            x = ffn_layer(shift_tokens(x), ln_g[i], ln_b[i], W1[i], b1[i], W2[i], b2[i]) + x
        return x
    x = L0_attn_hidden_states
    xn = _layernorm(x, axis=-1)
    x = x + _L0_attn_ref(xn, L0_attn_Wq, L0_attn_Wk, L0_attn_Wv, L0_attn_Wg, L0_attn_Wo, L0_attn_lepe_w, L0_attn_lepe_b) + _L0_ffn_ref(xn, L0_ffn_Wqkv, L0_ffn_q_scale, L0_ffn_k_scale, L0_ffn_Wo, L0_ffn_ln_g, L0_ffn_ln_b, L0_ffn_W1, L0_ffn_b1, L0_ffn_W2, L0_ffn_b2)
    return x

_drawn_inputs = setup_inputs


def setup_inputs(seed=0):
    import zlib

    import numpy as np

    out = dict(_drawn_inputs(seed))
    spreads = {'L0_attn_lepe_b': (0.0, 0.8),
     'L0_ffn_q_scale': (1.0, 0.6),
     'L0_ffn_k_scale': (1.0, 0.6),
     'L0_ffn_ln_g': (1.0, 0.6),
     'L0_ffn_ln_b': (0.0, 0.8),
     'L0_ffn_b1': (0.0, 0.8),
     'L0_ffn_b2': (0.0, 0.1)}
    factors = {'L0_attn_Wq': 8.0,
     'L0_attn_Wk': 8.0,
     'L0_attn_Wv': 8.0,
     'L0_attn_Wg': 8.0,
     'L0_attn_Wo': 8.0,
     'L0_attn_lepe_w': 8.0,
     'L0_ffn_W1': 3.641,
     'L0_ffn_W2': 3.573}
    for name, (base, spread) in spreads.items():
        noise = np.random.default_rng([zlib.crc32(name.encode()), seed]).standard_normal(out[name].shape)
        drawn = base * np.exp(spread * noise) if base else spread * noise
        out[name] = jnp.asarray(drawn.astype(out[name].dtype))
    for name, factor in factors.items():
        out[name] = (out[name] * factor).astype(out[name].dtype)
    return out
```

```python
from contextlib import ExitStack

import concourse.bass as bass
import numpy as np
from concourse import mybir

F32 = mybir.dt.float32
F32R = mybir.dt.float32r
BF16 = mybir.dt.bfloat16
ALU = mybir.AluOpType
ACT = mybir.ActivationFunctionType
AX = mybir.AxisListType

P = 128
S = 2048
D = 128
T = 512
G = S // T
C = T // P
NCH = S // P
W = 32
NW = P // W
DEPTH = 6
H = 16
DH = 64
HP = H // 2
INNER = H * DH
F = 341
FT = [(0, 128), (128, 128), (256, 85)]
KEYS = 2 * W
H1, DK = 8, 16
KLEPE = 5
NEG = -1e25
TINY = 1e-24
LN_EPS = 1e-5
QK_SCALE = 8.0
QS, QSR, KS, KSR, LG, LB, B1A, B1G, B2 = 0, 1, 2, 3, 4, 5, 6, 9, 12
NV = 13
WQ, WQR, WK, WKR, WV = 0, 1, 2, 3, 4


def constants():
    f32 = np.float32
    t = np.arange(S, dtype=f32)
    half = np.arange(0, DH, 2, dtype=f32)
    inv_freq = (f32(1.0) / f32(10000.0) ** (half / f32(DH))).astype(f32)
    freqs = (t[:, None] * inv_freq[None, :]).astype(f32)
    base = ((half + f32(0.4 * DH)) / f32(1.4 * DH)).astype(f32)
    scale = (base[None, :] ** ((t - S // 2) / (W // 2)).astype(f32)[:, None]).astype(f32)
    cos, sin = np.cos(freqs), np.sin(freqs)
    both = lambda a: np.concatenate([a, a], 1)
    sign = np.concatenate([-np.ones(DH // 2, f32), np.ones(DH // 2, f32)])[None, :]
    per_token = [both(cos * scale), both(sin * scale) * sign, both(cos / scale), both(sin / scale) * sign]
    rope = np.stack([np.concatenate([a.T, a.T], 0) for a in per_token], 1).astype(f32)
    rope = np.ascontiguousarray(rope.reshape(P, 4, G, T).transpose(2, 0, 1, 3))

    inv1 = (f32(1.0) / f32(10000.0) ** (np.arange(0, DK, 2, dtype=f32) / f32(DK))).astype(f32)
    fr1 = (t[:, None] * inv1[None, :]).astype(f32)
    c1, s1 = both(np.cos(fr1)), both(np.sin(fr1))
    s1[:, :DK // 2] *= -1
    rope1 = np.stack([c1, s1], 1).astype(f32).reshape(NCH, P, 2, DK).transpose(1, 0, 2, 3)

    a = np.arange(P) % W
    kk = np.arange(KEYS)
    seen = (kk[None, :] >= a[:, None]) & (kk[None, :] <= a[:, None] + W)
    first = seen & ~((np.arange(P)[:, None] < W) & (kk[None, :] < W))
    mask = np.where(np.stack([first] + [seen] * (G - 1), 1), 0.0, NEG)

    ind = np.zeros((P, HP, W), f32)
    sel = np.zeros((P, HP, P), f32)
    for j in range(HP):
        for h in range(2):
            ind[h * DH:(h + 1) * DH, j, 2 * (j // 4) + h] = 1
            sel[W * (j % 4) + 2 * (j // 4) + h, j, h * DH:(h + 1) * DH] = 1
    blk = (np.arange(P)[:, None] // DK == np.arange(P)[None, :] // DK).astype(f32)
    return {
        "c_rope": rope,
        "c_rope1": np.ascontiguousarray(rope1),
        "c_mask": mask.astype(f32),
        "c_ident": np.eye(P, dtype=f32),
        "c_ind": ind,
        "c_sel": sel,
        "c_blk": blk,
    }


def program(nc, a):
    with ExitStack() as ctx:
        def sb(name, shape, dt=F32):
            return ctx.enter_context(nc.sbuf_tensor(name, shape, dt))

        def sem(name):
            return ctx.enter_context(nc.semaphore(name))

        ps = ctx.enter_context(nc.psum_tensor("ps", [P, 8, 512], F32))

        XA = sb("XA", [P, S])
        XB = sb("XB", [P, T])
        CA = sb("CA", [P, G + 1])
        CB = sb("CB", [P, G + 1])
        rope = sb("rope", [P, 4, T])
        wh = sb("wh", [P, 5 * INNER], F32R)
        wl = sb("wl", [P, 5 * INNER], F32R)
        wo = sb("wo", [P, HP, D])
        w1h = sb("w1h", [P, 2 * F], F32R)
        w1l = sb("w1l", [P, 2 * F], F32R)
        w2 = sb("w2", [P, 3, D])
        vec = sb("vec", [P, NV])
        Kb = sb("Kb", [P, HP, W + T])
        Qb = sb("Qb", [P, HP, T])
        UV = sb("UV", [P, 2, 2, T])
        sq = sb("sq", [P, 4, T])
        xs = sb("xs", [P, T])
        xh = sb("xh", [P, T], F32R)
        xl = sb("xl", [P, T], F32R)
        Vs = sb("Vs", [P, C, 2, 512])
        V2 = sb("V2", [P, 4 * C + 1, 512])
        E = sb("E", [P, HP, 2, KEYS])
        Pr = sb("Pr", [P, HP, 2, KEYS])
        PT = sb("PT", [P, HP, P])
        On = sb("On", [P, HP, 2, DH])
        OT = sb("OT", [P, HP, P])
        R = sb("R", [P, T])
        Rh = sb("Rh", [P, T], F32R)
        Rl = sb("Rl", [P, T], F32R)
        rq = sb("rq", [P, C, 2, HP])
        mx = sb("mx", [P, HP, 2])
        rs = sb("rs", [P, HP, 2])
        ri = sb("ri", [P, HP, 2])
        mask = sb("mask", [P, G, KEYS], BF16)
        identb = sb("identb", [P, P], BF16)
        ident = sb("ident", [P, P])
        ind = sb("ind", [P, HP, W])
        sel = sb("sel", [P, HP, P], F32R)
        mean = sb("mean", [P, P])
        ln256 = sb("ln256", [P, 1])

        zn = On[:, :, :, :].rearrange("p j r k -> p (j r k)")[:, 0:T]
        Eflat = E[:, :, :, :].rearrange("p j r k -> p (j r k)")
        Prflat = Pr[:, :, :, :].rearrange("p j r k -> p (j r k)")
        Hh = [Eflat[:, 0:T], Eflat[:, T:2 * T], Prflat[:, 0:T]]

        Vflat = Vs[:, :, :, :].rearrange("p c h n -> p (c h n)")
        wraw = Vflat[:, 0:3 * INNER]
        w1raw = Vflat[:, 3 * INNER:3 * INNER + 2 * F]

        V2flat = V2[:, :, :].rearrange("p w n -> p (w n)")
        xt = V2flat[:, 0:S].rearrange("p (c n) -> p c n", c=NCH)
        xn = V2flat[:, S:2 * S].rearrange("p (c n) -> p c n", c=NCH)
        vT = V2flat[:, 2 * S:3 * S + KLEPE - 1]
        Qflat = Qb[:, :, :].rearrange("p j t -> p (j t)")
        qT = Qflat[:, 0:S]
        wb = Qflat[:, S:S + 5 * P]
        kvs = Qflat[:, S + 5 * P:S + 6 * P]
        ksb = Qflat[:, S + 6 * P:S + 7 * P]
        blk = Qflat[:, S + 7 * P:S + 8 * P]
        lw = Qflat[:, S + 8 * P:S + 8 * P + KLEPE + 1]
        ksum = Qflat[:, S + 8 * P + 8:S + 8 * P + 9]
        vsum = Qflat[:, S + 8 * P + 9:S + 8 * P + 10]
        rope1 = rope[:, 0, :].rearrange("p (c a n) -> p c a n", c=NCH, a=2)
        stats = Pr[:, 0:4, :, :].rearrange("p j r n -> p (j r n)")[:, 0:6 * NCH].rearrange("p (c n) -> p c n", c=NCH)
        mv = Pr[:, 4:8, :, :].rearrange("p j r n -> p (j r n)")[:, 0:2 * NCH].rearrange("p (c n) -> p c n", c=NCH)
        rstd1 = On[:, 0, 0, 0:NCH]

        def split(x):
            return x.rearrange("p (h s f) -> p h s f", s=2, f=DH // 2)

        raws = [split(wraw[:, i * INNER:(i + 1) * INNER]) for i in range(3)]
        weight_blocks = [(WK, raws[1]), (WKR, raws[1][:, :, ::-1, :]), (WV, raws[2]), (WQ, raws[0]),
                         (WQR, raws[0][:, :, ::-1, :])]

        SEMS = """const_in x_in b1_in scratch_out out_done
            bn_done mv_done rs1_done xn_done xT_done qkv1_done u1_done qk1_done v1_done kv_done kvs_done
            qTp_done qT_done vTp_done vT_done f1_done cv_done o1_done y1_done x1_done memset_done pool_set sel_done
            tab_in w_in wh_done wl_done vec_in xa_done xs_act xs_dve xh_done xl_done proj_done sq_done rope_mul rot_done
            norm_done rc_done ln_done r_done rhl_done rkb_done khat_done rqt_done rq_done vproj_done vs_done
            v2_slot v2_in k_halo s_done e_done m_done sub_done p_done rs_done ri_done pt_done pts_done o_done
            on_done ot_done ots_done wo_done xb_done z_act z_dve mu_done zc_done zsq_done var_done vare_done
            zln_done rstd_done zr_done zn_done zh_done zl_done h_done gelu_done hm_done w2_done
            fin_done fin_sum""".split()
        s = {name: sem(name) for name in SEMS}

        block = ctx.enter_context(nc.Block())

        @block.sync
        def _(e):
            e.dma_start(xt, a["x"].rearrange("(c p) n -> p c n", p=P)).then_inc(s["x_in"], 16)
            for dst, src in ((ident[:, :], a["c_ident"]), (Kb[:, 0:G, P:P + KEYS], a["c_mask"]),
                             (ind[:, :, :], a["c_ind"]), (Kb[:, :, 0:P], a["c_sel"])):
                e.dma_start(dst, src).then_inc(s["const_in"], 16)
            for i, name in enumerate(("Wq", "Wk", "Wv", "Wg", "Wo")):
                e.dma_start(wb[:, i * P:(i + 1) * P], a[name]).then_inc(s["b1_in"], 16)
            e.dma_start(blk, a["c_blk"]).then_inc(s["b1_in"], 16)
            e.dma_start(lw, a["lepe"]).then_inc(s["b1_in"], 16)
            e.dma_start(rope1, a["c_rope1"]).then_inc(s["b1_in"], 16)

            def layer_weights(l):
                e.dma_start(wraw, a["Wqkv"][bass.ds(l, 1)].rearrange("o p n -> p (o n)")).then_inc(s["w_in"], 16)
                e.dma_start(w1raw, a["W1"][bass.ds(l, 1)].rearrange("o p n -> p (o n)")).then_inc(s["w_in"], 16)

            layer_weights(0)
            e.wait_ge(s["x1_done"], G)
            e.dma_start(a["scratch"].rearrange("(c p) n -> p c n", p=P), xt).then_inc(s["scratch_out"], 16)
            e.wait_ge(s["scratch_out"], 16)

            with e.Fori(0, DEPTH) as l:
                e.wait_ge(s["xa_done"], l * G + G)
                e.dma_start(wo[:, :, :], a["Wo2"][bass.ds(l, 1)].rearrange("o p j n -> p (o j) n")).then_inc(s["vec_in"], 16)
                e.dma_start(w2[:, :, :], a["W2"][bass.ds(l, 1)].rearrange("o p j n -> p (o j) n")).then_inc(s["vec_in"], 16)
                e.dma_start(vec[:, :], a["vec"][bass.ds(l, 1)].rearrange("o p n -> p (o n)")).then_inc(s["vec_in"], 16)
                with e.Fori(0, G) as g:
                    n = l * G + g
                    e.wait_ge(s["xh_done"], n + 1)
                    e.dma_start(rope[:, :, :], a["c_rope"][bass.ds(g, 1)].rearrange("o p i t -> p (o i) t")).then_inc(s["tab_in"], 16)
                    e.wait_ge(s["vs_done"], n * C + C)
                    e.wait_ge(s["v2_slot"], n * 2 + 2)
                    for par in range(2):
                        for own in range(2):
                            for w in range(NW):
                                p0 = par * DH + own * W
                                first = w + 1 - own
                                e.dma_start(V2[p0:p0 + W, first:first + 4 * C - 3:4, :],
                                            Vs[w * W:(w + 1) * W, :, par, :]).then_inc(s["v2_in"], 16)
                e.wait_ge(s["v2_in"], (l * G + G) * 256)
                layer_weights(l + 1)
            e.wait_ge(s["xa_done"], (DEPTH + 1) * G)
            e.dma_start(xt, a["scratch"].rearrange("(c p) n -> p c n", p=P)).then_inc(s["scratch_out"], 16)
            out = a["out"].rearrange("(c p) n -> p c n", p=P)
            for g in range(G):
                e.wait_ge(s["fin_sum"], g + 1)
                e.dma_start(out[:, g * C:(g + 1) * C, :], xt[:, g * C:(g + 1) * C, :]).then_inc(s["out_done"], 16)
            e.wait_ge(s["out_done"], 16 * G)
            e.wait_ge(s["w_in"], 32 * (DEPTH + 1))

        @block.tensor
        def _(e):
            def mm(out, lhsT, rhs, start=True, stop=True, **kw):
                return e.matmul(out, lhsT, rhs, start=start, stop=stop, **kw)

            def mm3(out, hi, lo, mh, ml, start=True, stop=True):
                mm(out, hi, mh, start, False)
                mm(out, lo, mh, False, False)
                return mm(out, hi, ml, False, stop)


            e.wait_ge(s["const_in"], 64)
            e.wait_ge(s["memset_done"], 6)
            for g in range(G):
                for c in range(C):
                    e.wait_ge(s["xn_done"], g * C + c + 1)
                    ins = e.transpose(ps[:, g, c * P:(c + 1) * P], xn[:, g * C + c, :], ident[:, :])
                ins.then_inc(s["xT_done"], 1)
            e.wait_ge(s["b1_in"], 16 * 8)

            def kv_sums(c):
                e.wait_ge(s["qk1_done"], c + 1)
                e.wait_ge(s["v1_done"], c + 1)
                b = c % 2
                k_t = UV[:, b, 1, P:2 * P]
                v_t = sq[:, b, 0:P]
                mm(ps[:, 2, 0:P + 1], k_t, sq[:, b, 0:P + 1], c == 0, c == NCH - 1)
                mm(ps[:, 3, 0:1], v_t, sq[:, b, P:P + 1], c == 0, c == NCH - 1)
                if c >= 4 and c % 2 == 0:
                    e.wait_ge(s["qT_done"], c // 2 - 1)
                e.transpose(ps[:, 4 + (c // 2) % 2, (c % 2) * P:(c % 2 + 1) * P], UV[:, b, 1, 0:P],
                            ident[:, :]).then_inc(s["kv_done"], 1)

            e.wait_ge(s["xa_done"], G)
            for c in range(NCH):
                if c >= 2:
                    e.wait_ge(s["u1_done"], 3 * (c - 1))
                    e.wait_ge(s["v1_done"], c - 1)
                mm(ps[:, c % 2, 0:2 * P], XA[:, c * P:(c + 1) * P], wb[:, 0:2 * P])
                mm(ps[:, 6 + c % 2, 0:P], XA[:, c * P:(c + 1) * P], wb[:, 2 * P:3 * P]).then_inc(s["qkv1_done"], 1)
                if c >= 1:
                    kv_sums(c - 1)
            kv_sums(NCH - 1)
            e.wait_ge(s["u1_done"], 3 * NCH)
            e.wait_ge(s["v1_done"], NCH)
            for g in range(G):
                if g >= 2:
                    e.wait_ge(s["vT_done"], g - 1)
                mm(ps[:, g % 2, :], wb[:, 2 * P:3 * P], XA[:, g * T:(g + 1) * T]).then_inc(s["vTp_done"], 1)
            e.wait_ge(s["kvs_done"], 4)
            e.wait_ge(s["qT_done"], NCH // 2)
            for g in range(G):
                if g >= 1:
                    e.wait_ge(s["o1_done"], g)
                mm(ps[:, 4, :], wb[:, 3 * P:4 * P], XA[:, g * T:(g + 1) * T])
                mm(ps[:, 5, :], kvs, qT[:, g * T:(g + 1) * T])
                mm(ps[:, 6, :], ksb, qT[:, g * T:(g + 1) * T]).then_inc(s["f1_done"], 1)
                e.wait_ge(s["o1_done"], g + 1)
                if g >= 1:
                    e.wait_ge(s["x1_done"], g)
                for c in range(C):
                    ins = mm(ps[:, 7, c * P:(c + 1) * P], sq[:, 3, c * P:(c + 1) * P], wb[:, 4 * P:5 * P])
                ins.then_inc(s["y1_done"], 1)
            e.wait_ge(s["x1_done"], G)
            e.wait_ge(s["sel_done"], 3)

            with e.Fori(0, DEPTH) as l:
                with e.Fori(0, G) as g:
                    n = l * G + g
                    e.wait_ge(s["wh_done"], l * 6 + 6)
                    e.wait_ge(s["wl_done"], l * 6 + 6)
                    e.wait_ge(s["xh_done"], n + 1)
                    e.wait_ge(s["xl_done"], n + 1)

                    def qk_tile(t):
                        if t >= 2:
                            e.wait_ge(s["sq_done"], n * 16 + t - 1)
                            e.wait_ge(s["rope_mul"], n * 32 + 2 * (t - 1))
                        first = (WK if t < HP else WQ) * INNER + (t % HP) * P
                        for r in range(2):
                            c0 = first + r * INNER
                            ins = mm3(ps[:, 2 * (t % 2) + r, :], wh[:, c0:c0 + P], wl[:, c0:c0 + P], xh[:, :], xl[:, :])
                        ins.then_inc(s["proj_done"], 1)

                    def norms(q4):
                        e.wait_ge(s["sq_done"], n * 16 + 4 * q4 + 4)
                        if q4 == 2:
                            e.wait_ge(s["rc_done"], n * 2 + 1)
                        for i in range(4):
                            ins = mm(ps[i * W:(i + 1) * W, 6, :], ind[:, (4 * q4 + i) % HP, :], sq[:, i, :],
                                     q4 % 2 == 0, q4 % 2 == 1, tile_position=(0, i * W))
                        ins.then_inc(s["norm_done"], 1)

                    def v_chunk(c):
                        if c >= 1:
                            e.wait_ge(s["vs_done"], n * C + c)
                        for r in range(2):
                            rhs = lambda t: t[:, WV * INNER:].rearrange("p (j h f) -> p h j f", h=2, f=DH)[:, r]
                            ins = mm3(ps[:, 4 + r, :], xh[:, c * P:(c + 1) * P], xl[:, c * P:(c + 1) * P], rhs(wh), rhs(wl))
                        ins.then_inc(s["vproj_done"], 1)

                    def spread(j):
                        if j == 0:
                            e.wait_ge(s["rhl_done"], n * 2 + 2)
                        else:
                            e.wait_ge(s["khat_done"], n * HP + j)
                        mm(ps[:, 7, :], sel[:, j, :], Rh[:, :], True, False)
                        mm(ps[:, 7, :], sel[:, j, :], Rl[:, :], False, True).then_inc(s["rkb_done"], 1)

                    for t in range(2 * HP):
                        qk_tile(t)
                        if t in (4, 8, 12):
                            norms(t // 4 - 1)
                        if t in (2, 5, 7, 9):
                            v_chunk((2, 5, 7, 9).index(t))
                        if t >= 11:
                            spread(t - 11)
                    for j in range(5, HP):
                        spread(j)
                    norms(3)
                    e.wait_ge(s["r_done"], n * 2 + 2)
                    e.wait_ge(s["khat_done"], n * HP + HP)
                    for c in range(C):
                        ins = e.transpose(ps[:, 7, c * P:(c + 1) * P], R[:, c * P:(c + 1) * P], ident[:, :])
                    ins.then_inc(s["rqt_done"], 1)

                    def scores(c):
                        e.wait_ge(s["rot_done"], n * 16 + 16)
                        e.wait_ge(s["k_halo"], n + l + 2)
                        if c >= 1:
                            e.wait_ge(s["e_done"], n * C + c)
                        for r in range(2):
                            m = mask[:, bass.ds(g, 1), :] if c == 0 else mask[:, G - 1:G, :]
                            mm(ps[:, r, :].rearrange("p (j k) -> p j k", j=HP), identb[:, :],
                               m.broadcast_to([P, HP, KEYS]), True, False, skip_group_check=True)
                        for j in range(HP):
                            for r in range(2):
                                for w in range(NW):
                                    c0 = c * P + w * W
                                    rows = slice(r * DH, (r + 1) * DH)
                                    ins = mm(ps[w * W:(w + 1) * W, r, j * KEYS:(j + 1) * KEYS], Qb[rows, j, c0:c0 + W],
                                             Kb[rows, j, c0:c0 + KEYS], False, True, skip_group_check=True,
                                             tile_position=(r * DH, w * W))
                        ins.then_inc(s["s_done"], 1)

                    def transpose_p(c):
                        e.wait_ge(s["p_done"], n * C + c + 1)
                        for j in range(HP):
                            if c >= 2 and j % 4 == 0:
                                e.wait_ge(s["ots_done"], n * 8 + 2 * (c - 2) + j // 4 + 1)
                            ins = e.transpose(ps[:, 2 + j // 4, (j % 4) * P:(j % 4 + 1) * P],
                                              Pr[:, j, :, :], ident[:, :])
                            if j % 4 == 3:
                                ins.then_inc(s["pt_done"], 1)

                    def attend(c):
                        if c == 0:
                            e.wait_ge(s["v2_in"], n * 256 + 256)
                        else:
                            e.wait_ge(s["on_done"], n * C + c)
                        e.wait_ge(s["pts_done"], n * 8 + 2 * c + 2)
                        mm(ps[:, 4, 0:1], identb[:, :], identb[:, 0:1])
                        for j in range(HP):
                            for r in range(2):
                                for w in range(NW):
                                    rows = slice(r * DH, (r + 1) * DH)
                                    ins = mm(ps[w * W:(w + 1) * W, 4 + r, j * DH:(j + 1) * DH], PT[rows, j, w * W:(w + 1) * W],
                                             V2[rows, 4 * c + w, j * DH:(j + 1) * DH], tile_position=(r * DH, w * W))
                        ins.then_inc(s["o_done"], 1)

                    def out_proj(c):
                        e.wait_ge(s["on_done"], n * C + c + 1)
                        for j in range(HP):
                            if j % 4 == 0 and c < C - 1:
                                e.wait_ge(s["pts_done"], n * 8 + 2 * (c + 1) + j // 4 + 1)
                            ins = e.transpose(ps[:, 2 + j // 4, (j % 4) * P:(j % 4 + 1) * P],
                                              On[:, j, :, :], ident[:, :])
                            if j % 4 == 3:
                                ins.then_inc(s["ot_done"], 1)
                        e.wait_ge(s["ots_done"], n * 8 + 2 * c + 2)
                        for j in range(HP):
                            ins = mm(ps[:, 6, c * P:(c + 1) * P], wo[:, j, :], OT[:, j, :], j == 0, j == HP - 1)
                        ins.then_inc(s["wo_done"], 1)

                    e.wait_ge(s["vec_in"], l * 48 + 48)
                    scores(0)
                    scores(1)
                    for c in range(C):
                        transpose_p(c)
                        attend(c)
                        if c + 2 < C:
                            scores(c + 2)
                        if c >= 1:
                            out_proj(c - 1)
                    out_proj(C - 1)

                    e.wait_ge(s["z_act"], n * 2 + 2)
                    e.wait_ge(s["z_dve"], n * 2 + 2)
                    mm(ps[:, 7, :], mean[:, :], xs[:, :]).then_inc(s["mu_done"], 1)
                    e.wait_ge(s["zsq_done"], n + 1)
                    mm(ps[:, 6, :], mean[:, :], sq[:, 0, :]).then_inc(s["var_done"], 1)
                    e.wait_ge(s["zh_done"], n + 1)
                    e.wait_ge(s["zl_done"], n + 1)
                    for i, (f0, m) in enumerate(FT):
                        for r, c0 in ((0, F + f0), (1, f0)):
                            mm3(ps[0:m, 2 * i + r, :], w1h[:, c0:c0 + m], w1l[:, c0:c0 + m], xh[:, :],
                                xl[:, :]).then_inc(s["h_done"], 1)
                    for i, (f0, m) in enumerate(FT):
                        e.wait_ge(s["hm_done"], n * 3 + i + 1)
                        ins = mm(ps[:, 7, :], w2[0:m, i, :], Hh[i][0:m, :], i == 0, i == 2)
                    ins.then_inc(s["w2_done"], 1)

            e.wait_ge(s["xa_done"], (DEPTH + 1) * G)
            for g in range(G):
                for c in range(C):
                    ins = e.transpose(ps[:, g, c * P:(c + 1) * P], XA[:, (g * C + c) * P:(g * C + c + 1) * P], ident[:, :])
                ins.then_inc(s["fin_done"], 1)

        @block.vector
        def _(e):
            e.memset(mean[:, :], 1.0 / D).then_inc(s["memset_done"], 1)
            e.memset(CA[:, :], 0.0).then_inc(s["memset_done"], 1)
            e.memset(CB[:, :], 0.0).then_inc(s["memset_done"], 1)
            e.memset(sq[:, 0:2, P:P + 1], 1.0).then_inc(s["memset_done"], 1)
            e.memset(vT[:, 0:2], 0.0).then_inc(s["memset_done"], 1)
            e.memset(vT[:, S + 2:S + 4], 0.0).then_inc(s["memset_done"], 1)
            e.wait_ge(s["x_in"], 16)
            for c in range(NCH):
                e.bn_stats(stats[:, c, :], xt[:, c, :]).then_inc(s["bn_done"], 1)
            for c in range(NCH):
                e.wait_ge(s["bn_done"], c + 1)
                e.bn_aggr(mv[:, c, :], stats[:, c, :]).then_inc(s["mv_done"], 1)
            e.wait_ge(s["mv_done"], NCH)
            e.tensor_scalar(rstd1, mv[:, :, 1], LN_EPS, None, ALU.add).then_inc(s["mv_done"], 1)
            e.wait_ge(s["rs1_done"], 2)
            for c in range(NCH):
                e.tensor_scalar(xn[:, c, :], xt[:, c, :], mv[:, c, 0:1], rstd1[:, c:c + 1], ALU.subtract,
                                ALU.mult).then_inc(s["xn_done"], 1)
            e.wait_ge(s["const_in"], 64)
            e.tensor_copy(sel[:, :, :], Kb[:, :, 0:P]).then_inc(s["sel_done"], 1)
            e.tensor_copy(mask[:, :, :], Kb[:, 0:G, P:P + KEYS]).then_inc(s["sel_done"], 1)
            e.tensor_copy(identb[:, :], ident[:, :]).then_inc(s["sel_done"], 1)
            for g in range(G):
                e.wait_ge(s["xT_done"], g + 1)
                e.tensor_copy(XA[:, g * T:(g + 1) * T], ps[:, g, :]).then_inc(s["xa_done"], 1)
            e.wait_ge(s["b1_in"], 16 * 8)
            hd = DK // 2
            for c in range(NCH):
                e.wait_ge(s["qkv1_done"], c + 1)
                if c >= 2:
                    e.wait_ge(s["qk1_done"], c - 1)
                src = ps[:, c % 2, 0:2 * P].rearrange("p (h d) -> p h d", d=DK)
                u = UV[:, c % 2, 0, 0:2 * P].rearrange("p (h d) -> p h d", d=DK)
                v = UV[:, c % 2, 0, 2 * P:4 * P].rearrange("p (h d) -> p h d", d=DK)
                tab = lambda i, d0, d1: rope1[:, c, i:i + 1, d0:d1].broadcast_to([P, 2 * H1, d1 - d0])
                e.tensor_tensor(u, src, tab(0, 0, DK), ALU.mult).then_inc(s["u1_done"], 1)
                e.tensor_tensor(v[:, :, 0:hd], src[:, :, hd:DK], tab(1, 0, hd), ALU.mult).then_inc(s["u1_done"], 1)
                e.tensor_tensor(v[:, :, hd:DK], src[:, :, 0:hd], tab(1, hd, DK), ALU.mult).then_inc(s["u1_done"], 1)
                e.wait_ge(s["u1_done"], 3 * c + 3)
                if c >= 2:
                    e.wait_ge(s["kv_done"], c - 1)
                e.tensor_tensor(UV[:, c % 2, 1, 0:2 * P], UV[:, c % 2, 0, 0:2 * P], UV[:, c % 2, 0, 2 * P:4 * P],
                                ALU.add).then_inc(s["qk1_done"], 1)
            e.wait_ge(s["kv_done"], NCH)
            e.tensor_copy(ksum, ps[:, 2, P:P + 1]).then_inc(s["kvs_done"], 1)
            e.tensor_copy(vsum, ps[:, 3, 0:1]).then_inc(s["kvs_done"], 1)
            e.tensor_tensor(kvs, ps[:, 2, 0:P], blk, ALU.mult).then_inc(s["kvs_done"], 1)
            e.wait_ge(s["kvs_done"], 3)
            e.tensor_scalar(ksb, blk, ksum, None, ALU.mult).then_inc(s["kvs_done"], 1)
            e.wait_ge(s["vT_done"], G)
            acc, den, num, o1 = sq[:, 0, :], sq[:, 1, :], sq[:, 2, :], sq[:, 3, :]
            for g in range(G):
                k = g * (KLEPE + 5)
                e.tensor_scalar(acc, vT[:, g * T:g * T + T], lw[:, 0:1], lw[:, KLEPE:KLEPE + 1], ALU.mult,
                                ALU.add).then_inc(s["cv_done"], 1)
                for i in range(1, KLEPE):
                    e.wait_ge(s["cv_done"], k + i)
                    e.scalar_tensor_tensor(acc, vT[:, g * T + i:g * T + i + T], lw[:, i:i + 1], acc, ALU.mult,
                                           ALU.add).then_inc(s["cv_done"], 1)
                k += KLEPE
                e.wait_ge(s["f1_done"], g + 1)
                e.tensor_scalar(den, ps[:, 6, :], float(DK) ** -0.5, float(S), ALU.mult, ALU.add).then_inc(s["cv_done"], 1)
                e.tensor_scalar(num, ps[:, 5, :], float(DK) ** -0.5, None, ALU.mult).then_inc(s["cv_done"], 1)
                e.wait_ge(s["cv_done"], k + 1)
                e.reciprocal(den, den).then_inc(s["cv_done"], 1)
                e.wait_ge(s["cv_done"], k + 3)
                e.scalar_tensor_tensor(num, num, vsum, den, ALU.add, ALU.mult).then_inc(s["cv_done"], 1)
                e.wait_ge(s["cv_done"], k + 4)
                e.tensor_tensor(num, num, acc, ALU.add).then_inc(s["cv_done"], 1)
                e.wait_ge(s["cv_done"], k + 5)
                if g >= 1:
                    e.wait_ge(s["y1_done"], g)
                e.tensor_tensor(o1, ps[:, 4, :], num, ALU.mult).then_inc(s["o1_done"], 1)
                e.wait_ge(s["y1_done"], g + 1)
                xg = xt[:, g * C:(g + 1) * C, :]
                e.tensor_tensor(xg, ps[:, 7, :].rearrange("p (c n) -> p c n", c=C), xg, ALU.add).then_inc(s["x1_done"], 1)

            with e.Fori(0, DEPTH) as l:
                e.wait_ge(s["vec_in"], l * 48 + 48)
                for i, (b, src) in enumerate(weight_blocks):
                    e.wait_ge(s["wh_done"], l * 6 + i + 1)
                    o = slice(b * INNER, (b + 1) * INNER)
                    e.tensor_tensor(split(wl[:, o]), src, split(wh[:, o]), ALU.subtract).then_inc(s["wl_done"], 1)
                e.wait_ge(s["wh_done"], l * 6 + 6)
                e.tensor_tensor(w1l[:, :], w1raw, w1h[:, :], ALU.subtract).then_inc(s["wl_done"], 1)
                e.wait_ge(s["sel_done"], 3)
                e.wait_ge(s["vec_in"], l * 48 + 48)
                e.memset(Kb[:, :, T:T + W], 0.0).then_inc(s["k_halo"], 1)
                with e.Fori(0, G) as g:
                    n = l * G + g
                    e.wait_ge(s["xa_done"], n + 1)
                    e.wait_ge(s["k_halo"], n + l + 1)
                    e.tensor_copy(Kb[:, :, 0:W], Kb[:, :, T:T + W]).then_inc(s["k_halo"], 1)
                    e.tensor_copy(xs[D // 2:, 0:1], CA[D // 2:, bass.ds(g, 1)]).then_inc(s["xs_dve"], 1)
                    e.tensor_copy(CA[:, bass.ds(g + 1, 1)], XA[:, bass.ds(g * T + T - 1, 1)]).then_inc(s["xs_dve"], 1)
                    e.wait_ge(s["xh_done"], n + 1)
                    e.wait_ge(s["xs_dve"], n * 2 + 2)
                    e.tensor_tensor(xl[:, :], xs[:, :], xh[:, :], ALU.subtract).then_inc(s["xl_done"], 1)

                    def rope_tile(t):
                        e.wait_ge(s["proj_done"], n * 16 + t + 1)
                        if t >= 2:
                            e.wait_ge(s["rot_done"], n * 16 + t - 1)
                        for r in range(2):
                            v, i = (KS, 2) if t < HP else (QS, 0)
                            if r == 1:
                                e.wait_ge(s["sq_done"], n * 16 + t + 1)
                            e.scalar_tensor_tensor(UV[:, t % 2, r, :], ps[:, 2 * (t % 2) + r, :], vec[:, v + r:v + r + 1],
                                                   rope[:, i + r, :], ALU.mult, ALU.mult).then_inc(s["rope_mul"], 1)

                    def normalise_k(j):
                        e.wait_ge(s["rkb_done"], n * HP + j + 1)
                        e.wait_ge(s["rot_done"], n * 16 + j + 1)
                        kj = Kb[:, j, W:]
                        e.tensor_tensor(kj, ps[:, 7, :], kj, ALU.mult).then_inc(s["khat_done"], 1)

                    e.wait_ge(s["tab_in"], n * 16 + 16)
                    for t in range(2 * HP):
                        rope_tile(t)
                        if t == 8:
                            e.wait_ge(s["norm_done"], n * 4 + 2)
                            e.tensor_scalar(R[:, :], ps[:, 6, :], TINY, None, ALU.max).then_inc(s["rc_done"], 1)
                        if t == 10:
                            e.wait_ge(s["r_done"], n * 2 + 1)
                            e.tensor_copy(Rh[:, :], R[:, :]).then_inc(s["rhl_done"], 1)
                            e.wait_ge(s["rhl_done"], n * 2 + 1)
                            e.tensor_tensor(Rl[:, :], R[:, :], Rh[:, :], ALU.subtract).then_inc(s["rhl_done"], 1)
                        if t >= 11:
                            normalise_k(t - 11)
                    for j in range(5, HP):
                        normalise_k(j)
                    e.wait_ge(s["norm_done"], n * 4 + 4)
                    e.wait_ge(s["rhl_done"], n * 2 + 2)
                    e.tensor_scalar(R[:, :], ps[:, 6, :], TINY, None, ALU.max).then_inc(s["rc_done"], 1)
                    e.wait_ge(s["rqt_done"], n + 1)
                    rqt = ps[:, 7, :].rearrange("p (c q a r) -> p r c a q", c=C, q=4, r=2)
                    for r in range(2):
                        e.tensor_scalar(rq[:, :, r, :].rearrange("p c (a q) -> p c a q", a=2), rqt[:, r, :, 0:2, :],
                                        QK_SCALE, None, ALU.mult).then_inc(s["rq_done"], 1)

                    def banks(b0):
                        return ps[:, b0:b0 + 2, :].rearrange("p r (j k) -> p r j k", k=KEYS)

                    def parity_first(x):
                        return x.rearrange("p j r k -> p r j k")

                    def heads(x):
                        return x.rearrange("p j r k -> p (j r) k")

                    def scale_max(c):
                        e.wait_ge(s["s_done"], n * C + c + 1)
                        if c == 0:
                            e.wait_ge(s["rq_done"], n * 2 + 2)
                        else:
                            e.wait_ge(s["p_done"], n * C + c)
                        e.tensor_tensor(parity_first(E[:, :, :, :]), banks(0),
                                        rq[:, c].unsqueeze(3).broadcast_to([P, 2, HP, KEYS]), ALU.mult).then_inc(s["e_done"], 1)
                        e.wait_ge(s["e_done"], n * C + c + 1)
                        e.tensor_reduce(mx[:, :, :].rearrange("p j r -> p (j r)"), heads(E[:, :, :, :]), AX.X,
                                        ALU.max).then_inc(s["m_done"], 1)

                    def row_sums(c):
                        e.wait_ge(s["p_done"], n * C + c + 1)
                        e.tensor_reduce(rs[:, :, :].rearrange("p j r -> p (j r)"), heads(Pr[:, :, :, :]), AX.X,
                                        ALU.add).then_inc(s["rs_done"], 1)
                        e.wait_ge(s["rs_done"], n * C + c + 1)
                        e.reciprocal(ri[:, :, :], rs[:, :, :]).then_inc(s["ri_done"], 1)

                    def divide(c):
                        e.wait_ge(s["ri_done"], n * C + c + 1)
                        e.wait_ge(s["o_done"], n * C + c + 1)
                        if c >= 1:
                            e.wait_ge(s["ot_done"], n * 8 + 2 * c)
                        e.tensor_tensor(parity_first(On[:, :, :, :]), banks(4),
                                        ri[:, :, :].rearrange("p j r -> p r j").unsqueeze(3).broadcast_to([P, 2, HP, DH]),
                                        ALU.mult).then_inc(s["on_done"], 1)

                    for c in range(C):
                        scale_max(c)
                        if c >= 1:
                            divide(c - 1)
                            e.wait_ge(s["on_done"], n * C + c)
                        row_sums(c)
                    divide(C - 1)

                    e.wait_ge(s["wo_done"], n * C + C)
                    e.tensor_tensor(XB[:, :], ps[:, 6, :], XA[:, bass.ds(g * T, T)], ALU.add).then_inc(s["xb_done"], 1)
                    e.tensor_copy(xs[D // 2:, 0:1], CB[D // 2:, bass.ds(g, 1)]).then_inc(s["z_dve"], 1)
                    e.wait_ge(s["xb_done"], n + 1)
                    e.tensor_copy(CB[:, bass.ds(g + 1, 1)], XB[:, T - 1:T]).then_inc(s["z_dve"], 1)
                    e.wait_ge(s["mu_done"], n + 1)
                    e.tensor_tensor(zn, xs[:, :], ps[:, 7, :], ALU.subtract).then_inc(s["zc_done"], 1)
                    e.wait_ge(s["var_done"], n + 1)
                    e.tensor_scalar(R[:, :], ps[:, 6, :], LN_EPS, None, ALU.add).then_inc(s["vare_done"], 1)
                    e.wait_ge(s["rstd_done"], n + 1)
                    e.tensor_tensor(zn, zn, R[:, :], ALU.mult).then_inc(s["zr_done"], 1)
                    e.wait_ge(s["zr_done"], n + 1)
                    e.tensor_scalar(zn, zn, vec[:, LG:LG + 1], vec[:, LB:LB + 1], ALU.mult,
                                    ALU.add).then_inc(s["zn_done"], 1)
                    e.wait_ge(s["zh_done"], n + 1)
                    e.tensor_tensor(xl[:, :], zn, xh[:, :], ALU.subtract).then_inc(s["zl_done"], 1)
                    for i, (_, m) in enumerate(FT):
                        e.wait_ge(s["h_done"], n * 6 + 2 * i + 2)
                        e.wait_ge(s["gelu_done"], n * 3 + i + 1)
                        e.scalar_tensor_tensor(Hh[i][0:m, :], ps[0:m, 2 * i + 1, :], vec[0:m, B1A + i:B1A + i + 1],
                                               UV[0:m, i // 2, i % 2, :], ALU.add, ALU.mult).then_inc(s["hm_done"], 1)
                    e.wait_ge(s["w2_done"], n + 1)
                    e.scalar_tensor_tensor(XA[:, bass.ds(g * T, T)], ps[:, 7, :], vec[:, B2:B2 + 1], XB[:, :], ALU.add,
                                           ALU.add).then_inc(s["xa_done"], 1)

            e.wait_ge(s["scratch_out"], 32)
            for g in range(G):
                e.wait_ge(s["fin_done"], g + 1)
                xg = xt[:, g * C:(g + 1) * C, :]
                e.tensor_tensor(xg, ps[:, g, :].rearrange("p (c n) -> p c n", c=C), xg, ALU.add).then_inc(s["fin_sum"], 1)

        @block.scalar
        def _(e):
            def act(out, in_, f=ACT.Copy, **kw):
                return e.activation(out, in_, f, **kw)

            e.wait_ge(s["mv_done"], NCH + 1)
            act(rstd1, rstd1, ACT.Ln).then_inc(s["rs1_done"], 1)
            e.wait_ge(s["rs1_done"], 1)
            act(rstd1, rstd1, ACT.Exp, scale=-0.5).then_inc(s["rs1_done"], 1)
            e.wait_ge(s["memset_done"], 6)

            def q_transposed(pr):
                e.wait_ge(s["kv_done"], 2 * pr + 2)
                act(qT[:, pr * 2 * P:(pr + 1) * 2 * P], ps[:, 4 + pr % 2, 0:2 * P]).then_inc(s["qT_done"], 1)

            for c in range(NCH):
                e.wait_ge(s["qkv1_done"], c + 1)
                if c >= 2:
                    e.wait_ge(s["kv_done"], c - 1)
                act(sq[:, c % 2, 0:P], ps[:, 6 + c % 2, 0:P]).then_inc(s["v1_done"], 1)
                if c >= 3 and c % 2 == 1:
                    q_transposed(c // 2 - 1)
            q_transposed(NCH // 2 - 1)
            for g in range(G):
                e.wait_ge(s["vTp_done"], g + 1)
                act(vT[:, 2 + g * T:2 + (g + 1) * T], ps[:, g % 2, :]).then_inc(s["vT_done"], 1)

            with e.Fori(0, DEPTH) as l:
                e.wait_ge(s["w_in"], l * 32 + 32)
                e.wait_ge(s["vec_in"], l * 48 + 48)
                for b, src in weight_blocks:
                    act(split(wh[:, b * INNER:(b + 1) * INNER]), src).then_inc(s["wh_done"], 1)
                act(w1h[:, :], w1raw).then_inc(s["wh_done"], 1)
                with e.Fori(0, G) as g:
                    n = l * G + g
                    hf = D // 2
                    e.wait_ge(s["xa_done"], n + 1)
                    act(xs[0:hf, :], XA[0:hf, bass.ds(g * T, T)]).then_inc(s["xs_act"], 1)
                    act(xs[hf:, 1:T], XA[hf:, bass.ds(g * T, T - 1)]).then_inc(s["xs_act"], 1)
                    e.wait_ge(s["xs_act"], n * 2 + 2)
                    e.wait_ge(s["xs_dve"], n * 2 + 2)
                    act(xh[:, :], xs[:, :]).then_inc(s["xh_done"], 1)
                    e.wait_ge(s["pool_set"], 2)
                    e.wait_ge(s["scratch_out"], 16)
                    for p0 in (0, DH):
                        act(V2[p0:p0 + W, 0, :], V2[p0:p0 + W, 4 * C, :]).then_inc(s["v2_slot"], 1)

                    def square(t):
                        e.wait_ge(s["proj_done"], n * 16 + t + 1)
                        if t >= 4:
                            e.wait_ge(s["norm_done"], n * 4 + t // 4)
                        act(sq[:, t % 4, :], ps[:, 2 * (t % 2) + 1, :], ACT.Square).then_inc(s["sq_done"], 1)

                    def inverse_root(i):
                        e.wait_ge(s["rc_done"], n * 2 + i + 1)
                        act(R[:, :], R[:, :], ACT.Ln, scale=2.0 ** 16).then_inc(s["ln_done"], 1)
                        e.wait_ge(s["ln_done"], n * 2 + i + 1)
                        act(R[:, :], R[:, :], ACT.Exp, scale=-0.5, bias=ln256[:, 0:1]).then_inc(s["r_done"], 1)

                    for t in range(2 * HP):
                        square(t)
                        if t in (3, 6, 8, 10):
                            c = (3, 6, 8, 10).index(t)
                            e.wait_ge(s["vproj_done"], n * C + c + 1)
                            act(Vs[:, c, :, :], ps[:, 4:6, :]).then_inc(s["vs_done"], 1)
                        if t == 9:
                            inverse_root(0)
                    inverse_root(1)

                    def exponentials(c):
                        e.wait_ge(s["sub_done"], n * C + c + 1)
                        if c >= 1:
                            e.wait_ge(s["pt_done"], n * 8 + 2 * c)
                            e.wait_ge(s["rs_done"], n * C + c)
                        act(Pr[:, :, :, :], E[:, :, :, :], ACT.Exp).then_inc(s["p_done"], 1)

                    def p_out(c):
                        for i in range(2):
                            e.wait_ge(s["pt_done"], n * 8 + 2 * c + i + 1)
                            if c >= 1 and i == 0:
                                e.wait_ge(s["o_done"], n * C + c)
                            act(PT[:, 4 * i:4 * i + 4, :], ps[:, 2 + i, :]).then_inc(s["pts_done"], 1)

                    def o_out(c):
                        for i in range(2):
                            e.wait_ge(s["ot_done"], n * 8 + 2 * c + i + 1)
                            if c >= 1 and i == 0:
                                e.wait_ge(s["wo_done"], n * C + c)
                            act(OT[:, 4 * i:4 * i + 4, :], ps[:, 2 + i, :]).then_inc(s["ots_done"], 1)

                    for c in range(C):
                        exponentials(c)
                        if c >= 2:
                            o_out(c - 2)
                        p_out(c)
                    o_out(C - 2)
                    o_out(C - 1)

                    e.wait_ge(s["xb_done"], n + 1)
                    act(xs[0:hf, :], XB[0:hf, :]).then_inc(s["z_act"], 1)
                    act(xs[hf:, 1:T], XB[hf:, 0:T - 1]).then_inc(s["z_act"], 1)
                    e.wait_ge(s["zc_done"], n + 1)
                    act(sq[:, 0, :], zn, ACT.Square).then_inc(s["zsq_done"], 1)
                    e.wait_ge(s["vare_done"], n + 1)
                    act(R[:, :], R[:, :], ACT.Ln).then_inc(s["zln_done"], 1)
                    e.wait_ge(s["zln_done"], n + 1)
                    act(R[:, :], R[:, :], ACT.Exp, scale=-0.5).then_inc(s["rstd_done"], 1)
                    e.wait_ge(s["zn_done"], n + 1)
                    act(xh[:, :], zn).then_inc(s["zh_done"], 1)
                    for i, (_, m) in enumerate(FT):
                        e.wait_ge(s["h_done"], n * 6 + 2 * i + 1)
                        act(UV[0:m, i // 2, i % 2, :], ps[0:m, 2 * i, :], ACT.Gelu,
                            bias=vec[0:m, B1G + i:B1G + i + 1]).then_inc(s["gelu_done"], 1)

        @block.gpsimd
        def _(e):
            e.memset(V2[:, 4 * C, :], 0.0).then_inc(s["pool_set"], 1)
            e.memset(ln256[:, :], float(np.log(256.0))).then_inc(s["pool_set"], 1)
            with e.Fori(0, DEPTH) as l:
                with e.Fori(0, G) as g:
                    n = l * G + g
                    e.wait_ge(s["k_halo"], n + l + 2)
                    for t in range(2 * HP):
                        e.wait_ge(s["rope_mul"], n * 32 + 2 * t + 2)
                        dst = Kb[:, t, W:] if t < HP else Qb[:, t - HP, :]
                        e.tensor_tensor(dst, UV[:, t % 2, 0, :], UV[:, t % 2, 1, :], ALU.add).then_inc(s["rot_done"], 1)
                    for c in range(C):
                        e.wait_ge(s["m_done"], n * C + c + 1)
                        ev = E[:, :, :, :].rearrange("p j r k -> p (j r) k")
                        m = mx[:, :, :].rearrange("p j r -> p (j r)").unsqueeze(2).broadcast_to([P, H, KEYS])
                        e.tensor_tensor(ev, ev, m, ALU.subtract).then_inc(s["sub_done"], 1)


def kernel(**inputs):
    import numpy as _np
    import concourse.bacc as _bacc
    from concourse import mybir as _mybir
    from concourse.bass_utils import run_bass_kernel_spmd as _run

    inp = {k: _np.ascontiguousarray(v) for k, v in inputs.items()}
    A = lambda k: inp["L0_attn_" + k]
    B = lambda k: inp["L0_ffn_" + k]
    pad = lambda x: _np.concatenate([x, _np.zeros_like(x[:1])], 0)
    arrays = {"x": A("hidden_states").reshape(S, D)}
    for k in ("Wq", "Wk", "Wv", "Wg", "Wo"):
        arrays[k] = A(k).T
    arrays["lepe"] = _np.concatenate([A("lepe_w").reshape(D, KLEPE), A("lepe_b").reshape(D, 1)], 1)
    arrays["Wqkv"] = pad(B("Wqkv"))
    arrays["W1"] = pad(B("W1"))
    arrays["Wo2"] = B("Wo").reshape(DEPTH, HP, P, D).transpose(0, 2, 1, 3)
    w2 = _np.zeros((DEPTH, 3 * P, D), _np.float32)
    w2[:, :F] = B("W2")
    arrays["W2"] = w2.reshape(DEPTH, 3, P, D).transpose(0, 2, 1, 3)
    vec = _np.zeros((DEPTH, P, NV), _np.float32)
    rot = lambda x: _np.concatenate([x[:, DH // 2:], x[:, :DH // 2]], 1)
    for col, v in ((QS, B("q_scale")), (QSR, rot(B("q_scale"))), (KS, B("k_scale")), (KSR, rot(B("k_scale")))):
        vec[:, :, col] = _np.concatenate([v, v], 1)
    vec[:, :, LG], vec[:, :, LB], vec[:, :, B2] = B("ln_g"), B("ln_b"), B("b2")
    for i, (f0, m) in enumerate(FT):
        vec[:, :m, B1A + i] = B("b1")[:, f0:f0 + m]
        vec[:, :m, B1G + i] = B("b1")[:, F + f0:F + f0 + m]
    arrays["vec"] = vec
    arrays.update(constants())
    arrays = {k: _np.ascontiguousarray(v) for k, v in arrays.items()}

    nc = _bacc.Bacc("TRN2", target_bir_lowering=False, num_devices=1)
    aps = {k: nc.dram_tensor("in_" + k, v.shape, _mybir.dt.from_np(v.dtype), kind="ExternalInput").ap()
           for k, v in arrays.items()}
    aps["out"] = nc.dram_tensor("out_0", (S, D), _mybir.dt.float32, kind="ExternalOutput").ap()
    aps["scratch"] = nc.dram_tensor("scratch", (S, D), _mybir.dt.float32, kind="Internal").ap()
    program(nc, aps)
    r = _run(nc, [{"in_" + k: v for k, v in arrays.items()}], core_ids=[0])
    return r.results[0]["out_0"].reshape(1, S, D)
```

```python
from contextlib import ExitStack

import concourse.bass as bass
import numpy as np
from concourse import mybir

F32 = mybir.dt.float32
F32R = mybir.dt.float32r
BF16 = mybir.dt.bfloat16
ALU = mybir.AluOpType
ACT = mybir.ActivationFunctionType
AX = mybir.AxisListType

P = 128
S = 2048
D = 128
T = 256
G = S // T
C = T // P
NCH = S // P
T1 = 512
G1 = S // T1
C1 = T1 // P
W = 32
NW = P // W
DEPTH = 6
H = 16
DH = 64
HP = H // 2
INNER = H * DH
F = 341
FT = [(0, 128), (128, 128), (256, 85)]
KEYS = 2 * W
H1, DK = 8, 16
KLEPE = 5
NEG = -1e25
TINY = 1e-24
LN_EPS = 1e-5
QK_SCALE = 8.0
QS, QSR, KS, KSR = 0, 1, 2, 3
LG, LB, B1A, B1G, B2 = 0, 1, 2, 5, 8
WQ, WQR, WK, WKR, WV = 0, 1, 2, 3, 4

SCHEDULE = """c_wo a_xh a_wh0 a_xl a_wl0 a_wh1 a_wh2 a_wl1 a_wl2 b_rcq a_v0 a_vs0 c_xb c_xs b_lnq a_v1 a_vs1 c_mu c_zc
    b_s0 b_rqt b_rq b_scale0 a_slot a_wh3 c_zsq c_var c_vare c_rs a_wh4 a_qk0 a_sq0 b_max0 b_sub0 c_zn c_zh c_zl
    b_s1 b_exp0 a_wl3 a_wl4 a_mul0 a_qk1 a_sq1 a_rot0 a_rot1 b_scale1 a_mul1 b_sum0 b_max1 b_sub1 b_pt0 b_pto0
    a_norm0 a_qk2 a_sq2 a_mul2 a_rot2 a_rot3 b_att0 b_exp1 b_sum1 a_qk3 a_sq3 a_mul3 c_h0 c_gelu0 c_hm0 a_norm1
    b_div0 b_pt1 b_pto1 a_rck c_h1 c_gelu1 c_hm1 a_qk4 a_sq4 a_mul4 a_rot4 c_h2 c_gelu2 c_hm2 a_lnk a_rhl b_ot0
    b_oto0 a_qk5 a_sq5 a_mul5 a_rot5 b_att1 b_wo c_down a_kn0 c_fin a_sp0 a_sp1 b_xb a_kn1 b_div1 a_qk6 a_sq6
    a_mul6 a_rot6 b_ot1 b_oto1 a_sp2 a_norm2 a_kn2 a_sp3 a_kn3 a_qk7 a_sq7 a_mul7 a_rot7 a_norm3""".split()


def order(*stages):
    return [(x.rstrip("0123456789"), int(x[-1]) if x[-1].isdigit() else 0) for x in SCHEDULE if x[0] in stages]


def constants():
    f32 = np.float32
    t = np.arange(S, dtype=f32)
    half = np.arange(0, DH, 2, dtype=f32)
    inv_freq = (f32(1.0) / f32(10000.0) ** (half / f32(DH))).astype(f32)
    freqs = (t[:, None] * inv_freq[None, :]).astype(f32)
    base = ((half + f32(0.4 * DH)) / f32(1.4 * DH)).astype(f32)
    scale = (base[None, :] ** ((t - S // 2) / (W // 2)).astype(f32)[:, None]).astype(f32)
    cos, sin = np.cos(freqs), np.sin(freqs)
    both = lambda a: np.concatenate([a, a], 1)
    sign = np.concatenate([-np.ones(DH // 2, f32), np.ones(DH // 2, f32)])[None, :]
    per_token = [both(cos * scale), both(sin * scale) * sign, both(cos / scale), both(sin / scale) * sign]
    rope = np.stack([np.concatenate([a.T, a.T], 0) for a in per_token], 1).astype(f32)
    rope = np.ascontiguousarray(rope.reshape(P, 4, G, T).transpose(2, 0, 1, 3))

    inv1 = (f32(1.0) / f32(10000.0) ** (np.arange(0, DK, 2, dtype=f32) / f32(DK))).astype(f32)
    fr1 = (t[:, None] * inv1[None, :]).astype(f32)
    c1, s1 = both(np.cos(fr1)), both(np.sin(fr1))
    s1[:, :DK // 2] *= -1
    rope1 = np.stack([c1, s1], 1).astype(f32).reshape(NCH, P, 2, DK).transpose(1, 0, 2, 3)

    a = np.arange(P) % W
    kk = np.arange(KEYS)
    seen = (kk[None, :] >= a[:, None]) & (kk[None, :] <= a[:, None] + W)
    first = seen & ~((np.arange(P)[:, None] < W) & (kk[None, :] < W))
    mask = np.where(np.stack([first, seen], 1), 0.0, NEG)

    ind = np.zeros((P, HP, W), f32)
    sel = np.zeros((P, HP, P), f32)
    for j in range(HP):
        for h in range(2):
            ind[h * DH:(h + 1) * DH, j, 2 * (j // 4) + h] = 1
            sel[W * (j % 4) + 2 * (j // 4) + h, j, h * DH:(h + 1) * DH] = 1
    blk = (np.arange(P)[:, None] // DK == np.arange(P)[None, :] // DK).astype(f32)
    return {
        "c_rope": rope,
        "c_rope1": np.ascontiguousarray(rope1),
        "c_mask": mask.astype(f32),
        "c_ident": np.eye(P, dtype=f32),
        "c_ind": ind,
        "c_sel": sel,
        "c_blk": blk,
    }


def program(nc, a):
    with ExitStack() as ctx:
        def sb(name, shape, dt=F32):
            return ctx.enter_context(nc.sbuf_tensor(name, shape, dt))

        def sem(name):
            return ctx.enter_context(nc.semaphore(name))

        ps = ctx.enter_context(nc.psum_tensor("ps", [P, 8, 512], F32))

        XA = sb("XA", [P, 1 + S])
        XB = sb("XB", [P, 2, 1 + T])
        CB = sb("CB", [P, G + 1])
        rope = sb("rope", [P, 2, 4, T])
        wh = sb("wh", [P, 5 * INNER], F32R)
        wl = sb("wl", [P, 5 * INNER], F32R)
        wo = sb("wo", [P, HP, D])
        w1h = sb("w1h", [P, 2 * F], F32R)
        w1l = sb("w1l", [P, 2 * F], F32R)
        w2 = sb("w2", [P, 3, D])
        veca = sb("veca", [P, 4])
        vecc = sb("vecc", [P, 9])
        Kb = sb("Kb", [P, 2, HP, W + T])
        Qb = sb("Qb", [P, 2, HP, T])
        UV = sb("UV", [P, 2, 2, 2 * T])
        sq = sb("sq", [P, 4, 2 * T])
        xh = sb("xh", [P, 2, T], F32R)
        xl = sb("xl", [P, 2, T], F32R)
        raw = sb("raw", [P, 3 * INNER + 2 * F])
        V2 = sb("V2", [P, 2, 4 * C + 1, 512])
        E = sb("E", [P, C, HP, 2, KEYS])
        PT = sb("PT", [P, HP, P])
        On = sb("On", [P, HP, 2, DH])
        R = sb("R", [P, 2, T])
        Rh = sb("Rh", [P, T], F32R)
        Rl = sb("Rl", [P, T], F32R)
        rq = sb("rq", [P, C, 2, HP])
        mx = sb("mx", [P, C, HP, 2])
        rs = sb("rs", [P, C, HP, 2])
        ri = sb("ri", [P, C, HP, 2])
        zs = sb("zs", [P, T])
        zr = sb("zr", [P, T])
        zh = sb("zh", [P, T], F32R)
        zl = sb("zl", [P, T], F32R)
        hid = sb("hid", [P, 3, T])
        mask = sb("mask", [P, 2, KEYS], BF16)
        identb = sb("identb", [P, P], BF16)
        ident = sb("ident", [P, P])
        ind = sb("ind", [P, HP, W])
        sel = sb("sel", [P, HP, P], F32R)
        mean = sb("mean", [P, P])
        ln256 = sb("ln256", [P, 1])

        OT = On[:, :, :, :].rearrange("p j r k -> p j (r k)")
        zq = hid[:, 0, :]
        Vs = raw[:, INNER:INNER + C * INNER].rearrange("p (c h n) -> p c h n", c=C, h=2)
        wraw = raw[:, 0:3 * INNER]
        w1raw = raw[:, 3 * INNER:]

        NORM, FF = 6, 7

        V2flat = V2[:, :, :, :].rearrange("p a w n -> p (a w n)")
        xt = V2flat[:, 0:S].rearrange("p (c n) -> p c n", c=NCH)
        xn = V2flat[:, S:2 * S].rearrange("p (c n) -> p c n", c=NCH)
        vT = V2flat[:, 2 * S:3 * S + KLEPE - 1]
        Qflat = Qb[:, :, :, :].rearrange("p a j t -> p (a j t)")
        qT = Qflat[:, 0:S]
        wb = Qflat[:, S:S + 5 * P]
        kvs = Qflat[:, S + 5 * P:S + 6 * P]
        ksb = Qflat[:, S + 6 * P:S + 7 * P]
        blk = Qflat[:, S + 7 * P:S + 8 * P]
        lw = Qflat[:, S + 8 * P:S + 8 * P + KLEPE + 1]
        ksum = Qflat[:, S + 8 * P + 8:S + 8 * P + 9]
        vsum = Qflat[:, S + 8 * P + 9:S + 8 * P + 10]
        rope1 = rope[:, 0, :, :].rearrange("p i t -> p (i t)")[:, 0:NCH * 2 * DK].rearrange("p (c a n) -> p c a n", c=NCH, a=2)
        stats = E[:, 0, 0:4, :, :].rearrange("p j r n -> p (j r n)")[:, 0:6 * NCH].rearrange("p (c n) -> p c n", c=NCH)
        mv = E[:, 0, 4:8, :, :].rearrange("p j r n -> p (j r n)")[:, 0:2 * NCH].rearrange("p (c n) -> p c n", c=NCH)
        rstd1 = On[:, 0, 0, 0:NCH]

        def split(x):
            return x.rearrange("p (h s f) -> p h s f", s=2, f=DH // 2)

        raws = [split(wraw[:, i * INNER:(i + 1) * INNER]) for i in range(3)]
        weight_blocks = [(WV, raws[2]), (WK, raws[1]), (WKR, raws[1][:, :, ::-1, :]), (WQ, raws[0]),
                         (WQR, raws[0][:, :, ::-1, :])]

        SEMS = """const_in x_in b1_in scratch_out out_done
            bn_done mv_done rs1_done xn_done xT_done qkv1_done u1_done qk1_done v1_done kv_done kvs_done
            qT_done vTp_done vT_done f1_done cv_done o1_done y1_done x1_done memset_done pool_set sel_done
            tab_in w_in w1_in veca_in wo_in c_in wh_done wl_done w1h_done w1l_done xa_done xh_done xl_done proj_done
            sq_done rope_mul rot_done norm_done rc_done ln_done r_done rhl_done rkb_done khat_done rqt_done rq_done
            vproj_done vs_done v2_slot v2_in k_halo s_done e_done m_done sub_done p_done rs_done ri_done pt_done
            pts_done o_done on_done ot_done ots_done wo_done xb_done cb_done z_act mu_done zc_done zsq_done var_done
            vare_done zln_done rstd_done zr_done zn_done zh_done zl_done h_done gelu_done hm_done w2_done
            fin_done fin_sum""".split()
        s = {name: sem(name) for name in SEMS}

        block = ctx.enter_context(nc.Block())

        @block.sync
        def _(e):
            e.dma_start(xt, a["x"].rearrange("(c p) n -> p c n", p=P)).then_inc(s["x_in"], 16)
            for dst, src in ((ident[:, :], a["c_ident"]), (Kb[:, 0, 0:2, P:P + KEYS], a["c_mask"]),
                             (ind[:, :, :], a["c_ind"]), (Kb[:, 0, :, 0:P], a["c_sel"])):
                e.dma_start(dst, src).then_inc(s["const_in"], 16)
            for i, name in enumerate(("Wq", "Wk", "Wv", "Wg", "Wo")):
                e.dma_start(wb[:, i * P:(i + 1) * P], a[name]).then_inc(s["b1_in"], 16)
            e.dma_start(blk, a["c_blk"]).then_inc(s["b1_in"], 16)
            e.dma_start(lw, a["lepe"]).then_inc(s["b1_in"], 16)
            e.dma_start(rope1, a["c_rope1"]).then_inc(s["b1_in"], 16)

            def weights_a(l):
                e.dma_start(wraw, a["Wqkv"][bass.ds(l, 1)].rearrange("o p n -> p (o n)")).then_inc(s["w_in"], 16)

            def vectors_a(l):
                e.dma_start(veca[:, :], a["veca"][bass.ds(l, 1)].rearrange("o p n -> p (o n)")).then_inc(s["veca_in"], 16)

            def weights_b(l):
                e.dma_start(wo[:, :, :], a["Wo2"][bass.ds(l, 1)].rearrange("o p j n -> p (o j) n")).then_inc(s["wo_in"], 16)

            def weights_c(l):
                e.dma_start(w1raw, a["W1"][bass.ds(l, 1)].rearrange("o p n -> p (o n)")).then_inc(s["w1_in"], 16)
                e.dma_start(w2[:, :, :], a["W2"][bass.ds(l, 1)].rearrange("o p j n -> p (o j) n")).then_inc(s["c_in"], 16)
                e.dma_start(vecc[:, :], a["vecc"][bass.ds(l, 1)].rearrange("o p n -> p (o n)")).then_inc(s["c_in"], 16)

            def tables(m, g, parity, early=False):
                if not early:
                    e.wait_ge(s["rope_mul"], (m - 1) * 16)
                if not early or m == 1:
                    e.wait_ge(s["tab_in"], m * 16)
                e.dma_start(rope[:, parity, :, :],
                            a["c_rope"][bass.ds(g, 1)].rearrange("o p i t -> p (o i) t")).then_inc(s["tab_in"], 16)

            def windows(m, parity):
                e.wait_ge(s["v2_slot"], m * 2 + 2)
                e.wait_ge(s["vs_done"], m * 4 + 4)
                for par in range(2):
                    for own in range(2):
                        for w in range(NW):
                            p0 = par * DH + own * W
                            first = w + 1 - own
                            e.dma_start(V2[p0:p0 + W, parity, first:first + 4 * C - 3:4, :],
                                        Vs[w * W:(w + 1) * W, :, par, :]).then_inc(s["v2_in"], 16)

            weights_a(0)
            vectors_a(0)
            weights_b(0)
            weights_c(0)
            e.wait_ge(s["x1_done"], G1)
            e.dma_start(a["scratch"].rearrange("(c p) n -> p c n", p=P), xt).then_inc(s["scratch_out"], 16)
            e.wait_ge(s["scratch_out"], 16)
            tables(0, 0, 0, early=True)
            tables(1, 1, 1, early=True)
            windows(0, 0)
            windows(1, 1)
            with e.Fori(0, DEPTH) as l:
                with e.Fori(0, (G - 2) // 2) as h:
                    for i in range(2):
                        m = l * G + h * 2 + 2 + i
                        tables(m, h * 2 + 2 + i, i)
                        windows(m, i)
                e.wait_ge(s["v2_in"], (l * G + G) * 256)
                weights_a(l + 1)
                e.wait_ge(s["rope_mul"], (l * G + G) * 16)
                vectors_a(l + 1)
                for i in range(2):
                    m = l * G + G + i
                    tables(m, i, i)
                    if i == 1:
                        e.wait_ge(s["wo_done"], (l * G + G) * C)
                        weights_b(l + 1)
                    windows(m, i)
                e.wait_ge(s["xa_done"], l * G + 2 * G)
                weights_c(l + 1)
            e.wait_ge(s["v2_in"], (DEPTH * G + 2) * 256)
            e.wait_ge(s["o_done"], (DEPTH * G + 1) * C)
            e.dma_start(xt, a["scratch"].rearrange("(c p) n -> p c n", p=P)).then_inc(s["scratch_out"], 16)
            out = a["out"].rearrange("(c p) n -> p c n", p=P)
            for g in range(G1):
                e.wait_ge(s["fin_sum"], g + 1)
                e.dma_start(out[:, g * C1:(g + 1) * C1, :], xt[:, g * C1:(g + 1) * C1, :]).then_inc(s["out_done"], 16)
            e.wait_ge(s["out_done"], 16 * G1)
            for name, count in (("w_in", 1), ("veca_in", 1), ("wo_in", 1), ("w1_in", 1), ("c_in", 2)):
                e.wait_ge(s[name], 16 * count * (DEPTH + 1))

        def run(parts, step_a, step_b, step_c):
            stages = [stage for stage, step in zip("abc", (step_a, step_b, step_c)) if step]
            for name, i in order(*stages):
                if name in parts:
                    parts[name](i)

        def no_split(l, first):
            pass

        def engine_loop(e, iteration, first, split_c):
            first((0, 0, 0, 0, True))
            iteration((1, 1, 0, 1, False), (0, 0, 0, 0, True), None)
            split_c(0, True)
            with e.Fori(0, DEPTH) as l:
                with e.Fori(0, (G - 2) // 2) as h:
                    for i in range(2):
                        k = l * G + h * 2 + 1 + i
                        iteration((k + 1, h * 2 + 2 + i, l, i, False), (k, h * 2 + 1 + i, l, 1 - i, False),
                                  (k - 1, h * 2 + i, l, i, False))
                k = l * G + G - 1
                iteration((k + 1, 0, l + 1, 0, True), (k, G - 1, l, 1, False), (k - 1, G - 2, l, 0, False))
                iteration((k + 2, 1, l + 1, 1, False), (k + 1, 0, l + 1, 0, True), (k, G - 1, l, 1, False))
                split_c(l + 1, False)

        @block.tensor
        def _(e):
            def mm(out, lhsT, rhs, start=True, stop=True, **kw):
                return e.matmul(out, lhsT, rhs, start=start, stop=stop, **kw)

            def mm3(out, hi, lo, mh, ml, start=True, stop=True):
                mm(out, hi, mh, start, False)
                mm(out, lo, mh, False, False)
                return mm(out, hi, ml, False, stop)


            e.wait_ge(s["const_in"], 64)
            e.wait_ge(s["memset_done"], 6)
            for g in range(G1):
                for c in range(C1):
                    e.wait_ge(s["xn_done"], g * C1 + c + 1)
                    ins = e.transpose(ps[:, g, c * P:(c + 1) * P], xn[:, g * C1 + c, :], ident[:, :])
                ins.then_inc(s["xT_done"], 1)
            e.wait_ge(s["b1_in"], 16 * 8)

            def kv_sums(c):
                e.wait_ge(s["qk1_done"], c + 1)
                e.wait_ge(s["v1_done"], c + 1)
                b = c % 2
                k_t = UV[:, b, 1, P:2 * P]
                v_t = sq[:, b, 0:P]
                mm(ps[:, 2, 0:P + 1], k_t, sq[:, b, 0:P + 1], c == 0, c == NCH - 1)
                mm(ps[:, 3, 0:1], v_t, sq[:, b, P:P + 1], c == 0, c == NCH - 1)
                if c >= 4 and c % 2 == 0:
                    e.wait_ge(s["qT_done"], c // 2 - 1)
                e.transpose(ps[:, 4 + (c // 2) % 2, (c % 2) * P:(c % 2 + 1) * P], UV[:, b, 1, 0:P],
                            ident[:, :]).then_inc(s["kv_done"], 1)

            e.wait_ge(s["xa_done"], G)
            for c in range(NCH):
                if c >= 2:
                    e.wait_ge(s["u1_done"], 3 * (c - 1))
                    e.wait_ge(s["v1_done"], c - 1)
                mm(ps[:, c % 2, 0:2 * P], XA[:, 1 + c * P:1 + (c + 1) * P], wb[:, 0:2 * P])
                mm(ps[:, 6 + c % 2, 0:P], XA[:, 1 + c * P:1 + (c + 1) * P], wb[:, 2 * P:3 * P]).then_inc(s["qkv1_done"], 1)
                if c >= 1:
                    kv_sums(c - 1)
            kv_sums(NCH - 1)
            e.wait_ge(s["u1_done"], 3 * NCH)
            e.wait_ge(s["v1_done"], NCH)
            for g in range(G1):
                if g >= 2:
                    e.wait_ge(s["vT_done"], g - 1)
                mm(ps[:, g % 2, :], wb[:, 2 * P:3 * P], XA[:, 1 + g * T1:1 + (g + 1) * T1]).then_inc(s["vTp_done"], 1)
            e.wait_ge(s["kvs_done"], 4)
            e.wait_ge(s["qT_done"], NCH // 2)
            for g in range(G1):
                if g >= 1:
                    e.wait_ge(s["o1_done"], g)
                mm(ps[:, 4, :], wb[:, 3 * P:4 * P], XA[:, 1 + g * T1:1 + (g + 1) * T1])
                mm(ps[:, 5, :], kvs, qT[:, g * T1:(g + 1) * T1])
                mm(ps[:, 6, :], ksb, qT[:, g * T1:(g + 1) * T1]).then_inc(s["f1_done"], 1)
                e.wait_ge(s["o1_done"], g + 1)
                if g >= 1:
                    e.wait_ge(s["x1_done"], g)
                for c in range(C1):
                    ins = mm(ps[:, 7, c * P:(c + 1) * P], sq[:, 3, c * P:(c + 1) * P], wb[:, 4 * P:5 * P])
                ins.then_inc(s["y1_done"], 1)
            e.wait_ge(s["x1_done"], G1)
            e.wait_ge(s["sel_done"], 3)

            def iteration(step_a, step_b, step_c):
                if step_a:
                    m, _, la, pa, _ = step_a
                    first_a = isinstance(m, int) and m == 0
                if step_b:
                    n, _, lb, pb, layer_first = step_b
                    first_b = isinstance(n, int) and n == 0
                    Q, K, V = Qb[:, pb, :, :], Kb[:, pb, :, :], V2[:, pb, :, :]
                if step_c:
                    j, _, lc, pc, _ = step_c

                def a_v(c):
                    if c == 0:
                        e.wait_ge(s["xh_done"], m * 2 + 2)
                        e.wait_ge(s["xl_done"], m * 2 + 2)
                        e.wait_ge(s["wl_done"], la * 5 + 1)
                    for r in range(2):
                        if c == 1:
                            e.wait_ge(s["vs_done"], m * 4 + r + 1)
                        elif not first_a:
                            e.wait_ge(s["rope_mul"], m * 16 - 1 + r)
                        rhs = lambda t: t[:, WV * INNER:].rearrange("p (j h f) -> p h j f", h=2, f=DH)[:, r]
                        mm3(ps[:, r, :], xh[:, pa, c * P:(c + 1) * P], xl[:, pa, c * P:(c + 1) * P], rhs(wh),
                            rhs(wl)).then_inc(s["vproj_done"], 1)

                def a_qk(p):
                    for r in range(2):
                        if p in (0, HP // 2):
                            e.wait_ge(s["wl_done"], la * 5 + (2 if p == 0 else 4) + r)
                        if p == 0:
                            e.wait_ge(s["vs_done"], m * 4 + 3 + r)
                        elif p >= 6:
                            e.wait_ge(s["khat_done"], m * 4 + 2 * (p - 6) + r + 1)
                        else:
                            e.wait_ge(s["rope_mul"], m * 16 + 2 * (p - 1) + r + 1)
                        for i in range(2):
                            c0 = ((WK if p < HP // 2 else WQ) + r) * INNER + (2 * p + i) % HP * P
                            ins = mm3(ps[:, r, i * T:(i + 1) * T], wh[:, c0:c0 + P], wl[:, c0:c0 + P], xh[:, pa, :],
                                      xl[:, pa, :])
                        ins.then_inc(s["proj_done"], 1)

                def a_norm(q):
                    e.wait_ge(s["sq_done"], m * 8 + 2 * q + 2)
                    if q == 2:
                        e.wait_ge(s["rc_done"], m * 2 + 1)
                    elif q == 0 and not first_a:
                        e.wait_ge(s["rq_done"], m * 2)
                    for i in range(4):
                        ins = mm(ps[i * W:(i + 1) * W, NORM, q // 2 * T:(q // 2 + 1) * T], ind[:, (4 * q + i) % HP, :],
                                 sq[:, (2 * q + i // 2) % 4, i % 2 * T:(i % 2 + 1) * T], q % 2 == 0, q % 2 == 1,
                                 tile_position=(0, i * W))
                    ins.then_inc(s["norm_done"], 1)

                def a_sp(p):
                    if p == 0:
                        e.wait_ge(s["rhl_done"], m * 2 + 2)
                    e.wait_ge(s["rope_mul"], m * 16 + (11, 12, 13, 14)[p])
                    for i in range(2):
                        out = ps[:, p % 2, i * T:(i + 1) * T]
                        mm(out, sel[:, 2 * p + i, :], Rh[:, :], True, False)
                        ins = mm(out, sel[:, 2 * p + i, :], Rl[:, :], False, True)
                    ins.then_inc(s["rkb_done"], 1)

                def b_rqt(_):
                    e.wait_ge(s["r_done"], n * 2 + 2)
                    for c in range(C):
                        ins = e.transpose(ps[:, NORM, T + c * P:T + (c + 1) * P], R[:, 1, c * P:(c + 1) * P], ident[:, :])
                    ins.then_inc(s["rqt_done"], 1)

                def b_s(c):
                    if c == 0:
                        e.wait_ge(s["rot_done"], n * 8 + 8)
                        e.wait_ge(s["khat_done"], n * 4 + 4)
                        e.wait_ge(s["k_halo"], n + 1)
                        if not first_b:
                            e.wait_ge(s["on_done"], n * C)
                    else:
                        e.wait_ge(s["e_done"], n * C + c)
                    chosen = 0 if layer_first and c == 0 else 1
                    for r in range(2):
                        mm(ps[:, 2 + r, :].rearrange("p (j k) -> p j k", j=HP), identb[:, :],
                           mask[:, chosen:chosen + 1, :].broadcast_to([P, HP, KEYS]), True, False, skip_group_check=True)
                    for h in range(HP):
                        for r in range(2):
                            for w in range(NW):
                                c0 = c * P + w * W
                                rows = slice(r * DH, (r + 1) * DH)
                                ins = mm(ps[w * W:(w + 1) * W, 2 + r, h * KEYS:(h + 1) * KEYS], Q[rows, h, c0:c0 + W],
                                         K[rows, h, c0:c0 + KEYS], False, True, skip_group_check=True,
                                         tile_position=(r * DH, w * W))
                    ins.then_inc(s["s_done"], 1)

                def transposed(src, done):
                    for h in range(HP):
                        ins = e.transpose(ps[:, 4 + h // 4, (h % 4) * P:(h % 4 + 1) * P], src[:, h, :, :], ident[:, :])
                        if h % 4 == 3:
                            ins.then_inc(s[done], 1)

                def b_pt(c):
                    e.wait_ge(s["p_done"], n * C + c + 1)
                    if c == 1:
                        e.wait_ge(s["pts_done"], n * 4 + 2)
                    elif not first_b:
                        e.wait_ge(s["xb_done"], n * C)
                    transposed(E[:, c], "pt_done")

                def b_att(c):
                    if c == 0:
                        e.wait_ge(s["v2_in"], n * 256 + 256)
                        e.wait_ge(s["e_done"], n * C + C)
                    else:
                        e.wait_ge(s["on_done"], n * C + c)
                    e.wait_ge(s["pts_done"], n * 4 + 2 * c + 2)
                    mm(ps[:, 2, 0:1], identb[:, :], identb[:, 0:1])
                    for h in range(HP):
                        for r in range(2):
                            for w in range(NW):
                                rows = slice(r * DH, (r + 1) * DH)
                                ins = mm(ps[w * W:(w + 1) * W, 2 + r, h * DH:(h + 1) * DH], PT[rows, h, w * W:(w + 1) * W],
                                         V[rows, 4 * c + w, h * DH:(h + 1) * DH], tile_position=(r * DH, w * W))
                    ins.then_inc(s["o_done"], 1)

                def b_ot(c):
                    e.wait_ge(s["on_done"], n * C + c + 1)
                    if c == 0:
                        e.wait_ge(s["pts_done"], n * 4 + 4)
                    else:
                        e.wait_ge(s["xb_done"], n * C + c)
                    transposed(On[:, :, :, :], "ot_done")

                def out_proj(step, layer, c):
                    if c == 0:
                        e.wait_ge(s["wo_in"], layer * 16 + 16)
                    e.wait_ge(s["ots_done"], step * 4 + 2 * c + 2)
                    for h in range(HP):
                        ins = mm(ps[:, 4, 0:P], wo[:, h, :], OT[:, h, :], h == 0, h == HP - 1)
                    ins.then_inc(s["wo_done"], 1)

                def b_wo(_):
                    out_proj(n, lb, 0)

                def c_wo(_):
                    out_proj(j, lc, 1)

                def c_mu(_):
                    e.wait_ge(s["z_act"], j * 2 + 2)
                    e.wait_ge(s["xa_done"], j + G)
                    mm(ps[:, FF, 0:T], mean[:, :], zs[:, :]).then_inc(s["mu_done"], 1)

                def c_var(_):
                    e.wait_ge(s["zsq_done"], j + 1)
                    mm(ps[:, FF, T:2 * T], mean[:, :], zq[:, :]).then_inc(s["var_done"], 1)

                def c_h(i):
                    f0, width = FT[i]
                    if i == 0:
                        e.wait_ge(s["zh_done"], j + 1)
                        e.wait_ge(s["zl_done"], j + 1)
                        e.wait_ge(s["w1l_done"], lc + 1)
                    else:
                        e.wait_ge(s["hm_done"], j * 3 + i)
                    for r, c0 in ((0, F + f0), (1, f0)):
                        ins = mm3(ps[0:width, FF, r * T:(r + 1) * T], w1h[:, c0:c0 + width], w1l[:, c0:c0 + width],
                                  zh[:, :], zl[:, :])
                    ins.then_inc(s["h_done"], 1)

                def c_down(_):
                    e.wait_ge(s["hm_done"], j * 3 + 3)
                    e.wait_ge(s["c_in"], lc * 32 + 32)
                    for i, (_, width) in enumerate(FT):
                        ins = mm(ps[:, FF, 0:T], w2[0:width, i, :], hid[0:width, i, :], i == 0, i == 2)
                    ins.then_inc(s["w2_done"], 1)

                parts = {"a_v": a_v, "a_qk": a_qk, "a_norm": a_norm, "a_sp": a_sp, "b_rqt": b_rqt, "b_s": b_s,
                         "b_pt": b_pt, "b_att": b_att, "b_ot": b_ot, "b_wo": b_wo, "c_wo": c_wo, "c_mu": c_mu, "c_var": c_var,
                         "c_h": c_h, "c_down": c_down}
                run(parts, step_a, step_b, step_c)

            engine_loop(e, iteration, lambda step: iteration(step, None, None), no_split)

            e.wait_ge(s["xa_done"], (DEPTH + 1) * G)
            e.wait_ge(s["rope_mul"], (DEPTH * G + 2) * 16)
            e.wait_ge(s["khat_done"], (DEPTH * G + 2) * 4)
            e.wait_ge(s["on_done"], (DEPTH * G + 1) * C)
            for g in range(G1):
                for c in range(C1):
                    ins = e.transpose(ps[:, g, c * P:(c + 1) * P], XA[:, 1 + (g * C1 + c) * P:1 + (g * C1 + c + 1) * P], ident[:, :])
                ins.then_inc(s["fin_done"], 1)

        @block.vector
        def _(e):
            e.memset(mean[:, :], 1.0 / D).then_inc(s["memset_done"], 1)
            e.memset(XA[:, 0:1], 0.0).then_inc(s["memset_done"], 1)
            e.memset(CB[:, :], 0.0).then_inc(s["memset_done"], 1)
            e.memset(sq[:, 0:2, P:P + 1], 1.0).then_inc(s["memset_done"], 1)
            e.memset(vT[:, 0:2], 0.0).then_inc(s["memset_done"], 1)
            e.memset(vT[:, S + 2:S + 4], 0.0).then_inc(s["memset_done"], 1)
            e.wait_ge(s["x_in"], 16)
            for c in range(NCH):
                e.bn_stats(stats[:, c, :], xt[:, c, :]).then_inc(s["bn_done"], 1)
            for c in range(NCH):
                e.wait_ge(s["bn_done"], c + 1)
                e.bn_aggr(mv[:, c, :], stats[:, c, :]).then_inc(s["mv_done"], 1)
            e.wait_ge(s["mv_done"], NCH)
            e.tensor_scalar(rstd1, mv[:, :, 1], LN_EPS, None, ALU.add).then_inc(s["mv_done"], 1)
            e.wait_ge(s["rs1_done"], 2)
            for c in range(NCH):
                e.tensor_scalar(xn[:, c, :], xt[:, c, :], mv[:, c, 0:1], rstd1[:, c:c + 1], ALU.subtract,
                                ALU.mult).then_inc(s["xn_done"], 1)
            e.wait_ge(s["const_in"], 64)
            e.tensor_copy(sel[:, :, :], Kb[:, 0, :, 0:P]).then_inc(s["sel_done"], 1)
            e.tensor_copy(mask[:, :, :], Kb[:, 0, 0:2, P:P + KEYS]).then_inc(s["sel_done"], 1)
            e.tensor_copy(identb[:, :], ident[:, :]).then_inc(s["sel_done"], 1)
            for g in range(G1):
                e.wait_ge(s["xT_done"], g + 1)
                e.tensor_copy(XA[:, 1 + g * T1:1 + (g + 1) * T1], ps[:, g, :]).then_inc(s["xa_done"], 2)
            e.wait_ge(s["b1_in"], 16 * 8)
            hd = DK // 2
            for c in range(NCH):
                e.wait_ge(s["qkv1_done"], c + 1)
                if c >= 2:
                    e.wait_ge(s["qk1_done"], c - 1)
                src = ps[:, c % 2, 0:2 * P].rearrange("p (h d) -> p h d", d=DK)
                u = UV[:, c % 2, 0, 0:2 * P].rearrange("p (h d) -> p h d", d=DK)
                v = UV[:, c % 2, 0, 2 * P:4 * P].rearrange("p (h d) -> p h d", d=DK)
                tab = lambda i, d0, d1: rope1[:, c, i:i + 1, d0:d1].broadcast_to([P, 2 * H1, d1 - d0])
                e.tensor_tensor(u, src, tab(0, 0, DK), ALU.mult).then_inc(s["u1_done"], 1)
                e.tensor_tensor(v[:, :, 0:hd], src[:, :, hd:DK], tab(1, 0, hd), ALU.mult).then_inc(s["u1_done"], 1)
                e.tensor_tensor(v[:, :, hd:DK], src[:, :, 0:hd], tab(1, hd, DK), ALU.mult).then_inc(s["u1_done"], 1)
                e.wait_ge(s["u1_done"], 3 * c + 3)
                if c >= 2:
                    e.wait_ge(s["kv_done"], c - 1)
                e.tensor_tensor(UV[:, c % 2, 1, 0:2 * P], UV[:, c % 2, 0, 0:2 * P], UV[:, c % 2, 0, 2 * P:4 * P],
                                ALU.add).then_inc(s["qk1_done"], 1)
            e.wait_ge(s["kv_done"], NCH)
            e.tensor_copy(ksum, ps[:, 2, P:P + 1]).then_inc(s["kvs_done"], 1)
            e.tensor_copy(vsum, ps[:, 3, 0:1]).then_inc(s["kvs_done"], 1)
            e.tensor_tensor(kvs, ps[:, 2, 0:P], blk, ALU.mult).then_inc(s["kvs_done"], 1)
            e.wait_ge(s["kvs_done"], 3)
            e.tensor_scalar(ksb, blk, ksum, None, ALU.mult).then_inc(s["kvs_done"], 1)
            e.wait_ge(s["vT_done"], G1)
            acc, den, num, o1 = sq[:, 0, :], sq[:, 1, :], sq[:, 2, :], sq[:, 3, :]
            for g in range(G1):
                k = g * (KLEPE + 5)
                e.tensor_scalar(acc, vT[:, g * T1:g * T1 + T1], lw[:, 0:1], lw[:, KLEPE:KLEPE + 1], ALU.mult,
                                ALU.add).then_inc(s["cv_done"], 1)
                for i in range(1, KLEPE):
                    e.wait_ge(s["cv_done"], k + i)
                    e.scalar_tensor_tensor(acc, vT[:, g * T1 + i:g * T1 + i + T1], lw[:, i:i + 1], acc, ALU.mult,
                                           ALU.add).then_inc(s["cv_done"], 1)
                k += KLEPE
                e.wait_ge(s["f1_done"], g + 1)
                e.tensor_scalar(den, ps[:, 6, :], float(DK) ** -0.5, float(S), ALU.mult, ALU.add).then_inc(s["cv_done"], 1)
                e.tensor_scalar(num, ps[:, 5, :], float(DK) ** -0.5, None, ALU.mult).then_inc(s["cv_done"], 1)
                e.wait_ge(s["cv_done"], k + 1)
                e.reciprocal(den, den).then_inc(s["cv_done"], 1)
                e.wait_ge(s["cv_done"], k + 3)
                e.scalar_tensor_tensor(num, num, vsum, den, ALU.add, ALU.mult).then_inc(s["cv_done"], 1)
                e.wait_ge(s["cv_done"], k + 4)
                e.tensor_tensor(num, num, acc, ALU.add).then_inc(s["cv_done"], 1)
                e.wait_ge(s["cv_done"], k + 5)
                if g >= 1:
                    e.wait_ge(s["y1_done"], g)
                e.tensor_tensor(o1, ps[:, 4, :], num, ALU.mult).then_inc(s["o1_done"], 1)
                e.wait_ge(s["y1_done"], g + 1)
                xg = xt[:, g * C1:(g + 1) * C1, :]
                e.tensor_tensor(xg, ps[:, 7, :].rearrange("p (c n) -> p c n", c=C1), xg, ALU.add).then_inc(s["x1_done"], 1)

            def iteration(step_a, step_b, step_c):
                if step_a:
                    m, ga, la, pa, layer_first = step_a
                    first_a = isinstance(m, int) and m == 0
                    early = isinstance(m, int)
                if step_b:
                    n, gb, _, pb, _ = step_b
                    first_b = isinstance(n, int) and n == 0
                if step_c:
                    j, gc, lc, pc, _ = step_c
                hf = D // 2

                def a_wl(i):
                    if layer_first and not first_a:
                        e.wait_ge(s["wh_done"], la * 5 + i + 1)
                        b, src = weight_blocks[i]
                        o = slice(b * INNER, (b + 1) * INNER)
                        e.tensor_tensor(split(wl[:, o]), src, split(wh[:, o]), ALU.subtract).then_inc(s["wl_done"], 1)

                def a_xl(_):
                    e.wait_ge(s["xh_done"], m * 2 + 2)
                    if not early:
                        e.wait_ge(s["proj_done"], (m - 1) * 16)
                    e.tensor_tensor(xl[0:hf, pa, :], XA[0:hf, bass.ds(ga * T + 1, T)], xh[0:hf, pa, :],
                                    ALU.subtract).then_inc(s["xl_done"], 1)
                    e.tensor_tensor(xl[hf:, pa, :], XA[hf:, bass.ds(ga * T, T)], xh[hf:, pa, :],
                                    ALU.subtract).then_inc(s["xl_done"], 1)
                    if not early:
                        e.wait_ge(s["s_done"], (m - 1) * C)
                    if first_a:
                        e.wait_ge(s["sel_done"], 3)
                    if layer_first:
                        e.memset(Kb[:, pa, :, 0:W], 0.0).then_inc(s["k_halo"], 1)
                    else:
                        e.wait_ge(s["khat_done"], m * 4)
                        e.tensor_copy(Kb[:, pa, :, 0:W], Kb[:, 1 - pa, :, T:T + W]).then_inc(s["k_halo"], 1)

                def a_mul(p):
                    if p == 0:
                        e.wait_ge(s["tab_in"], m * 16 + 16)
                        e.wait_ge(s["veca_in"], la * 16 + 16)
                    if p >= 2:
                        e.wait_ge(s["rot_done"], m * 8 + p - 1)
                    elif not first_a:
                        e.wait_ge(s["rot_done"], m * 8)
                    v, i = (KS, 2) if p < HP // 2 else (QS, 0)
                    for r in range(2):
                        if r == 0:
                            e.wait_ge(s["proj_done"], m * 16 + 2 * p + 1)
                        else:
                            e.wait_ge(s["sq_done"], m * 8 + p + 1)
                        e.scalar_tensor_tensor(UV[:, p % 2, r, :].rearrange("p (i t) -> p i t", i=2),
                                               ps[:, r, :].rearrange("p (i t) -> p i t", i=2), veca[:, v + r:v + r + 1],
                                               rope[:, pa, i + r:i + r + 1, :].broadcast_to([P, 2, T]), ALU.mult,
                                               ALU.mult).then_inc(s["rope_mul"], 1)

                def clamp(step, side):
                    e.wait_ge(s["norm_done"], step * 4 + 2 * side + 2)
                    if not (isinstance(step, int) and step == 0):
                        e.wait_ge(s["rqt_done"], step)
                    e.tensor_scalar(R[:, side, :], ps[:, NORM, side * T:(side + 1) * T], TINY, None,
                                    ALU.max).then_inc(s["rc_done"], 1)

                def a_rck(_):
                    clamp(m, 0)

                def b_rcq(_):
                    clamp(n, 1)

                def a_rhl(_):
                    e.wait_ge(s["r_done"], m * 2 + 1)
                    if not first_a:
                        e.wait_ge(s["rkb_done"], m * 4)
                    e.tensor_copy(Rh[:, :], R[:, 0, :]).then_inc(s["rhl_done"], 1)
                    e.wait_ge(s["rhl_done"], m * 2 + 1)
                    e.tensor_tensor(Rl[:, :], R[:, 0, :], Rh[:, :], ALU.subtract).then_inc(s["rhl_done"], 1)

                def a_kn(p):
                    e.wait_ge(s["rkb_done"], m * 4 + p + 1)
                    e.wait_ge(s["rot_done"], m * 8 + p + 1)
                    k = Kb[:, pa, 2 * p:2 * p + 2, W:]
                    e.tensor_tensor(k, ps[:, p % 2, :].rearrange("p (i t) -> p i t", i=2), k,
                                    ALU.mult).then_inc(s["khat_done"], 1)

                def b_rq(_):
                    e.wait_ge(s["rqt_done"], n + 1)
                    rqt = ps[:, NORM, T:T + C * P].rearrange("p (c q a r) -> p r c a q", c=C, q=4, r=2)
                    for r in range(2):
                        e.tensor_scalar(rq[:, :, r, :].rearrange("p c (a q) -> p c a q", a=2), rqt[:, r, :, 0:2, :],
                                        QK_SCALE, None, ALU.mult).then_inc(s["rq_done"], 1)

                def banks():
                    return ps[:, 2:4, :].rearrange("p r (j k) -> p r j k", k=KEYS)

                def parity_first(x):
                    return x.rearrange("p j r k -> p r j k")

                def heads(x):
                    return x.rearrange("p j r k -> p (j r) k")

                def b_scale(c):
                    e.wait_ge(s["s_done"], n * C + c + 1)
                    if c == 0:
                        e.wait_ge(s["rq_done"], n * 2 + 2)
                        if not first_b:
                            e.wait_ge(s["pt_done"], n * 4)
                    e.tensor_tensor(parity_first(E[:, c]), banks(),
                                    rq[:, c].unsqueeze(3).broadcast_to([P, 2, HP, KEYS]), ALU.mult).then_inc(s["e_done"], 1)

                def b_max(c):
                    e.wait_ge(s["e_done"], n * C + c + 1)
                    e.tensor_reduce(mx[:, c].rearrange("p j r -> p (j r)"), heads(E[:, c]), AX.X,
                                    ALU.max).then_inc(s["m_done"], 1)

                def b_sum(c):
                    e.wait_ge(s["p_done"], n * C + c + 1)
                    e.tensor_reduce(rs[:, c].rearrange("p j r -> p (j r)"), heads(E[:, c]), AX.X,
                                    ALU.add).then_inc(s["rs_done"], 1)
                    e.wait_ge(s["rs_done"], n * C + c + 1)
                    e.reciprocal(ri[:, c], rs[:, c]).then_inc(s["ri_done"], 1)

                def b_div(c):
                    e.wait_ge(s["ri_done"], n * C + c + 1)
                    e.wait_ge(s["o_done"], n * C + c + 1)
                    if c >= 1 or not first_b:
                        e.wait_ge(s["wo_done"], n * C + c)
                    e.tensor_tensor(parity_first(On[:, :, :, :]), banks(),
                                    ri[:, c].rearrange("p j r -> p r j").unsqueeze(3).broadcast_to([P, 2, HP, DH]),
                                    ALU.mult).then_inc(s["on_done"], 1)

                def residual(step, g, parity, c):
                    e.wait_ge(s["wo_done"], step * C + c + 1)
                    if c == 0 and not first_b:
                        e.wait_ge(s["cb_done"], step * 2)
                    e.tensor_tensor(XB[:, parity, 1 + c * P:1 + (c + 1) * P], ps[:, 4, 0:P],
                                    XA[:, bass.ds(g * T + c * P + 1, P)], ALU.add).then_inc(s["xb_done"], 1)
                    if c == 0:
                        e.tensor_copy(XB[:, parity, 0:1], CB[:, bass.ds(g, 1)]).then_inc(s["cb_done"], 1)
                    else:
                        e.wait_ge(s["xb_done"], step * C + C)
                        e.tensor_copy(CB[:, bass.ds(g + 1, 1)], XB[:, parity, T:T + 1]).then_inc(s["cb_done"], 1)

                def b_xb(_):
                    residual(n, gb, pb, 0)

                def c_xb(_):
                    residual(j, gc, pc, 1)

                def c_zc(_):
                    e.wait_ge(s["mu_done"], j + 1)
                    e.tensor_tensor(zs[:, :], zs[:, :], ps[:, FF, 0:T], ALU.subtract).then_inc(s["zc_done"], 1)

                def c_vare(_):
                    e.wait_ge(s["var_done"], j + 1)
                    e.tensor_scalar(zr[:, :], ps[:, FF, T:2 * T], LN_EPS, None, ALU.add).then_inc(s["vare_done"], 1)

                def c_zn(_):
                    e.wait_ge(s["rstd_done"], j + 1)
                    e.tensor_tensor(zs[:, :], zs[:, :], zr[:, :], ALU.mult).then_inc(s["zr_done"], 1)
                    e.wait_ge(s["zr_done"], j + 1)
                    e.wait_ge(s["c_in"], lc * 32 + 32)
                    e.tensor_scalar(zs[:, :], zs[:, :], vecc[:, LG:LG + 1], vecc[:, LB:LB + 1], ALU.mult,
                                    ALU.add).then_inc(s["zn_done"], 1)

                def c_zl(_):
                    e.wait_ge(s["zh_done"], j + 1)
                    e.tensor_tensor(zl[:, :], zs[:, :], zh[:, :], ALU.subtract).then_inc(s["zl_done"], 1)

                def c_hm(i):
                    width = FT[i][1]
                    e.wait_ge(s["gelu_done"], j * 3 + i + 1)
                    e.scalar_tensor_tensor(hid[0:width, i, :], ps[0:width, FF, T:2 * T], vecc[0:width, B1A + i:B1A + i + 1],
                                           hid[0:width, i, :], ALU.add, ALU.mult).then_inc(s["hm_done"], 1)

                def c_fin(_):
                    e.wait_ge(s["w2_done"], j + 1)
                    e.scalar_tensor_tensor(XA[:, bass.ds(gc * T + 1, T)], ps[:, FF, 0:T], vecc[:, B2:B2 + 1],
                                           XB[:, pc, 1:], ALU.add, ALU.add).then_inc(s["xa_done"], 1)

                parts = {"a_wl": a_wl, "a_xl": a_xl, "a_mul": a_mul, "a_rck": a_rck, "b_rcq": b_rcq, "a_rhl": a_rhl, "a_kn": a_kn,
                         "b_rq": b_rq, "b_scale": b_scale, "b_max": b_max, "b_sum": b_sum, "b_div": b_div, "b_xb": b_xb, "c_xb": c_xb,
                         "c_zc": c_zc, "c_vare": c_vare, "c_zn": c_zn, "c_zl": c_zl, "c_hm": c_hm, "c_fin": c_fin}
                run(parts, step_a, step_b, step_c)

            def split_c(l, first):
                e.wait_ge(s["w1h_done"], l + 1)
                e.tensor_tensor(w1l[:, :], w1raw, w1h[:, :], ALU.subtract).then_inc(s["w1l_done"], 1)

            engine_loop(e, iteration, lambda step: iteration(step, None, None), split_c)

            e.wait_ge(s["scratch_out"], 32)
            for g in range(G1):
                e.wait_ge(s["fin_done"], g + 1)
                xg = xt[:, g * C1:(g + 1) * C1, :]
                e.tensor_tensor(xg, ps[:, g, :].rearrange("p (c n) -> p c n", c=C1), xg, ALU.add).then_inc(s["fin_sum"], 1)

        @block.scalar
        def _(e):
            def act(out, in_, f=ACT.Copy, **kw):
                return e.activation(out, in_, f, **kw)

            def logarithm_and_exponential():
                e.preload_act_table_set("natural_log_exp_and_others")

            logarithm_and_exponential()
            e.wait_ge(s["mv_done"], NCH + 1)
            act(rstd1, rstd1, ACT.Ln).then_inc(s["rs1_done"], 1)
            e.wait_ge(s["rs1_done"], 1)
            act(rstd1, rstd1, ACT.Exp, scale=-0.5).then_inc(s["rs1_done"], 1)
            e.wait_ge(s["memset_done"], 6)

            def high_parts(i):
                b, src = weight_blocks[i]
                act(split(wh[:, b * INNER:(b + 1) * INNER]), src).then_inc(s["wh_done"], 1)

            e.wait_ge(s["w_in"], 16)
            for i in range(len(weight_blocks)):
                high_parts(i)

            def q_transposed(pr):
                e.wait_ge(s["kv_done"], 2 * pr + 2)
                act(qT[:, pr * 2 * P:(pr + 1) * 2 * P], ps[:, 4 + pr % 2, 0:2 * P]).then_inc(s["qT_done"], 1)

            for c in range(NCH):
                e.wait_ge(s["qkv1_done"], c + 1)
                if c >= 2:
                    e.wait_ge(s["kv_done"], c - 1)
                act(sq[:, c % 2, 0:P], ps[:, 6 + c % 2, 0:P]).then_inc(s["v1_done"], 1)
                if c >= 3 and c % 2 == 1:
                    q_transposed(c // 2 - 1)
            q_transposed(NCH // 2 - 1)
            for g in range(G1):
                e.wait_ge(s["vTp_done"], g + 1)
                act(vT[:, 2 + g * T1:2 + (g + 1) * T1], ps[:, g % 2, :]).then_inc(s["vT_done"], 1)

            def iteration(step_a, step_b, step_c):
                if step_a:
                    m, ga, la, pa, layer_first = step_a
                    first_a = isinstance(m, int) and m == 0
                    early = isinstance(m, int)
                if step_b:
                    n, _, _, pb, _ = step_b
                    first_b = isinstance(n, int) and n == 0
                if step_c:
                    j, _, lc, pc, _ = step_c
                hf = D // 2

                def a_wh(i):
                    if layer_first and not first_a:
                        if i == 0:
                            e.wait_ge(s["w_in"], la * 16 + 16)
                            e.wait_ge(s["proj_done"], m * 16)
                            e.wait_ge(s["wl_done"], la * 5)
                        high_parts(i)

                def a_xh(_):
                    e.wait_ge(s["xa_done"], m + 1)
                    if not early:
                        e.wait_ge(s["proj_done"], (m - 1) * 16)
                        e.wait_ge(s["xl_done"], (m - 1) * 2)
                    act(xh[0:hf, pa, :], XA[0:hf, bass.ds(ga * T + 1, T)]).then_inc(s["xh_done"], 1)
                    act(xh[hf:, pa, :], XA[hf:, bass.ds(ga * T, T)]).then_inc(s["xh_done"], 1)

                def a_slot(_):
                    if first_a:
                        e.wait_ge(s["pool_set"], 2)
                        e.wait_ge(s["scratch_out"], 16)
                    else:
                        e.wait_ge(s["v2_in"], m * 256)
                    if not early:
                        e.wait_ge(s["o_done"], (m - 1) * C)
                    for p0 in (0, DH):
                        act(V2[p0:p0 + W, pa, 0, :], V2[p0:p0 + W, 1 - pa, 4 * C, :]).then_inc(s["v2_slot"], 1)

                def a_vs(c):
                    if c == 0:
                        e.wait_ge(s["wl_done"], la * 5 + 3)
                        if not first_a:
                            e.wait_ge(s["v2_in"], m * 256)
                    for r in range(2):
                        e.wait_ge(s["vproj_done"], m * 4 + 2 * c + r + 1)
                        act(Vs[:, c, r, :], ps[:, r, :]).then_inc(s["vs_done"], 1)

                def a_sq(p):
                    e.wait_ge(s["proj_done"], m * 16 + 2 * p + 2)
                    if p >= 4:
                        e.wait_ge(s["norm_done"], m * 4 + (p - 4) // 2 + 1)
                    elif not first_a:
                        e.wait_ge(s["norm_done"], m * 4)
                    act(sq[:, p % 4, :], ps[:, 1, :], ACT.Square).then_inc(s["sq_done"], 1)

                def inverse_root(step, side):
                    e.wait_ge(s["rc_done"], step * 2 + side + 1)
                    act(R[:, side, :], R[:, side, :], ACT.Ln, scale=2.0 ** 16).then_inc(s["ln_done"], 1)
                    e.wait_ge(s["ln_done"], step * 2 + side + 1)
                    act(R[:, side, :], R[:, side, :], ACT.Exp, scale=-0.5, bias=ln256[:, 0:1]).then_inc(s["r_done"], 1)

                def a_lnk(_):
                    inverse_root(m, 0)

                def b_lnq(_):
                    inverse_root(n, 1)

                def b_exp(c):
                    e.wait_ge(s["sub_done"], n * C + c + 1)
                    act(E[:, c], E[:, c], ACT.Exp).then_inc(s["p_done"], 1)

                def b_pto(c):
                    for i in range(2):
                        e.wait_ge(s["pt_done"], n * 4 + 2 * c + i + 1)
                        if i == 0 and (c >= 1 or not first_b):
                            e.wait_ge(s["o_done"], n * C + c)
                        act(PT[:, 4 * i:4 * i + 4, :], ps[:, 4 + i, :]).then_inc(s["pts_done"], 1)

                def b_oto(c):
                    for i in range(2):
                        e.wait_ge(s["ot_done"], n * 4 + 2 * c + i + 1)
                        act(OT[:, 4 * i:4 * i + 4, :], ps[:, 4 + i, :]).then_inc(s["ots_done"], 1)

                def c_xs(_):
                    e.wait_ge(s["xb_done"], j * C + C)
                    e.wait_ge(s["cb_done"], j * 2 + 1)
                    act(zs[0:hf, :], XB[0:hf, pc, 1:]).then_inc(s["z_act"], 1)
                    act(zs[hf:, :], XB[hf:, pc, 0:T]).then_inc(s["z_act"], 1)

                def c_zsq(_):
                    e.wait_ge(s["zc_done"], j + 1)
                    act(zq[:, :], zs[:, :], ACT.Square).then_inc(s["zsq_done"], 1)

                def c_rs(_):
                    e.wait_ge(s["vare_done"], j + 1)
                    act(zr[:, :], zr[:, :], ACT.Ln).then_inc(s["zln_done"], 1)
                    e.wait_ge(s["zln_done"], j + 1)
                    act(zr[:, :], zr[:, :], ACT.Exp, scale=-0.5).then_inc(s["rstd_done"], 1)

                def c_zh(_):
                    e.wait_ge(s["zn_done"], j + 1)
                    act(zh[:, :], zs[:, :]).then_inc(s["zh_done"], 1)

                def c_gelu(i):
                    width = FT[i][1]
                    e.wait_ge(s["h_done"], j * 3 + i + 1)
                    act(hid[0:width, i, :], ps[0:width, FF, 0:T], ACT.Gelu,
                        bias=vecc[0:width, B1G + i:B1G + i + 1]).then_inc(s["gelu_done"], 1)
                    if i == 2:
                        logarithm_and_exponential()

                parts = {"a_wh": a_wh, "a_xh": a_xh, "a_slot": a_slot, "a_vs": a_vs, "a_sq": a_sq, "a_lnk": a_lnk, "b_lnq": b_lnq, "b_exp": b_exp,
                         "b_pto": b_pto, "b_oto": b_oto, "c_xs": c_xs, "c_zsq": c_zsq, "c_rs": c_rs, "c_zh": c_zh,
                         "c_gelu": c_gelu}
                run(parts, step_a, step_b, step_c)

            def split_c(l, first):
                e.wait_ge(s["w1_in"], l * 16 + 16)
                e.wait_ge(s["c_in"], l * 32 + 32)
                if not first:
                    e.wait_ge(s["w1l_done"], l)
                act(w1h[:, :], w1raw).then_inc(s["w1h_done"], 1)

            engine_loop(e, iteration, lambda step: iteration(step, None, None), split_c)

        @block.gpsimd
        def _(e):
            e.memset(V2[:, 1, 4 * C, :], 0.0).then_inc(s["pool_set"], 1)
            e.memset(ln256[:, :], float(np.log(256.0))).then_inc(s["pool_set"], 1)
            for i, (b, src) in enumerate(weight_blocks):
                e.wait_ge(s["wh_done"], i + 1)
                o = slice(b * INNER, (b + 1) * INNER)
                e.tensor_tensor(split(wl[:, o]), src, split(wh[:, o]), ALU.subtract).then_inc(s["wl_done"], 1)

            def iteration(step_a, step_b, step_c):
                if step_a:
                    m, _, _, pa, _ = step_a
                    early = isinstance(m, int)
                if step_b:
                    n, _, _, _, _ = step_b

                def a_rot(p):
                    if p == 0:
                        e.wait_ge(s["k_halo"], m + 1)
                        if not early:
                            e.wait_ge(s["s_done"], (m - 1) * C)
                    e.wait_ge(s["rope_mul"], m * 16 + 2 * p + 2)
                    dst = Kb[:, pa, 2 * p:2 * p + 2, W:] if p < HP // 2 else Qb[:, pa, 2 * p - HP:2 * p - HP + 2, :]
                    u, v = (UV[:, p % 2, r, :].rearrange("p (i t) -> p i t", i=2) for r in range(2))
                    e.tensor_tensor(dst, u, v, ALU.add).then_inc(s["rot_done"], 1)

                def b_sub(c):
                    e.wait_ge(s["m_done"], n * C + c + 1)
                    ev = E[:, c].rearrange("p j r k -> p (j r) k")
                    largest = mx[:, c].rearrange("p j r -> p (j r)").unsqueeze(2).broadcast_to([P, H, KEYS])
                    e.tensor_tensor(ev, ev, largest, ALU.subtract).then_inc(s["sub_done"], 1)

                run({"a_rot": a_rot, "b_sub": b_sub}, step_a, step_b, step_c)

            engine_loop(e, iteration, lambda step: iteration(step, None, None), no_split)


def kernel(**inputs):
    import numpy as _np
    import concourse.bacc as _bacc
    from concourse import mybir as _mybir
    from concourse.bass_utils import run_bass_kernel_spmd as _run

    inp = {k: _np.ascontiguousarray(v) for k, v in inputs.items()}
    A = lambda k: inp["L0_attn_" + k]
    B = lambda k: inp["L0_ffn_" + k]
    pad = lambda x: _np.concatenate([x, _np.zeros_like(x[:1])], 0)
    arrays = {"x": A("hidden_states").reshape(S, D)}
    for k in ("Wq", "Wk", "Wv", "Wg", "Wo"):
        arrays[k] = A(k).T
    arrays["lepe"] = _np.concatenate([A("lepe_w").reshape(D, KLEPE), A("lepe_b").reshape(D, 1)], 1)
    arrays["Wqkv"] = pad(B("Wqkv"))
    arrays["W1"] = pad(B("W1"))
    arrays["Wo2"] = pad(B("Wo")).reshape(DEPTH + 1, HP, P, D).transpose(0, 2, 1, 3)
    w2 = _np.zeros((DEPTH + 1, 3 * P, D), _np.float32)
    w2[:DEPTH, :F] = B("W2")
    arrays["W2"] = w2.reshape(DEPTH + 1, 3, P, D).transpose(0, 2, 1, 3)
    veca = _np.zeros((DEPTH + 1, P, 4), _np.float32)
    vecc = _np.zeros((DEPTH + 1, P, 9), _np.float32)
    rot = lambda x: _np.concatenate([x[:, DH // 2:], x[:, :DH // 2]], 1)
    for col, v in ((QS, B("q_scale")), (QSR, rot(B("q_scale"))), (KS, B("k_scale")), (KSR, rot(B("k_scale")))):
        veca[:DEPTH, :, col] = _np.concatenate([v, v], 1)
    vecc[:DEPTH, :, LG], vecc[:DEPTH, :, LB], vecc[:DEPTH, :, B2] = B("ln_g"), B("ln_b"), B("b2")
    for i, (f0, m) in enumerate(FT):
        vecc[:DEPTH, :m, B1A + i] = B("b1")[:, f0:f0 + m]
        vecc[:DEPTH, :m, B1G + i] = B("b1")[:, F + f0:F + f0 + m]
    arrays["veca"], arrays["vecc"] = veca, vecc
    arrays.update(constants())
    arrays = {k: _np.ascontiguousarray(v) for k, v in arrays.items()}

    nc = _bacc.Bacc("TRN2", target_bir_lowering=False, num_devices=1)
    aps = {k: nc.dram_tensor("in_" + k, v.shape, _mybir.dt.from_np(v.dtype), kind="ExternalInput").ap()
           for k, v in arrays.items()}
    aps["out"] = nc.dram_tensor("out_0", (S, D), _mybir.dt.float32, kind="ExternalOutput").ap()
    aps["scratch"] = nc.dram_tensor("scratch", (S, D), _mybir.dt.float32, kind="Internal").ap()
    program(nc, aps)
    r = _run(nc, [{"in_" + k: v for k, v in arrays.items()}], core_ids=[0])
    return r.results[0]["out_0"].reshape(1, S, D)
```
